# Optimizing a Trainium2 kernel written in Bass

```python
import numpy as np
import jax
import jax.numpy as jnp

def _softmax(x, axis=-1):
    return jax.nn.softmax(x, axis=axis)

def _gelu(x):
    return jax.nn.gelu(x, approximate=True)

def _silu(x):
    return jax.nn.silu(x)

def _sigmoid(x):
    return jax.nn.sigmoid(x)

def _layernorm(x, axis=-1, eps=1e-05):
    m = jnp.mean(x, axis=axis, keepdims=True)
    v = jnp.var(x, axis=axis, keepdims=True)
    return (x - m) / jnp.sqrt(v + eps)

def _scatter_add(tgt, idx, src, axis=0):
    return tgt.at[idx].add(src)

def _segment_sum(src, seg, n):
    return jax.ops.segment_sum(src, seg, n)
kernel_name = 'mk_gnn_ffn_d2_gnn_r8_869d02'

def setup_inputs(seed: int=0):
    np.random.seed(seed)
    _w = jnp.asarray

    def _rec_inputs():
        import jax
        import jax.numpy as jnp
        _gk = jax.random.key(seed)
        x = -0.0003713 + 1 * jax.random.normal(jax.random.fold_in(_gk, 1), (6250, 256), jnp.float32)
        _s = jax.random.randint(jax.random.fold_in(_gk, 2), (50000,), 0, 6250, jnp.int32)
        _d = jax.random.randint(jax.random.fold_in(_gk, 3), (50000,), 0, 6250, jnp.int32)
        _loop = jnp.arange(6250, dtype=jnp.int32)
        src = jnp.concatenate([_s, _d, _loop])
        dst = jnp.concatenate([_d, _s, _loop])
        _o = jnp.argsort(dst, stable=True)
        src = src[_o]
        dst = dst[_o]
        edge_attr_32 = 0.000189758 + 1.00013 * jax.random.normal(jax.random.fold_in(_gk, 12), (106250, 32), jnp.float32)
        return (x, src, dst, edge_attr_32)
    x, src, dst, edge_attr_32 = _rec_inputs()

    def _L0_gnn_setup():
        import jax, jax.numpy as jnp
        import numpy as np
        N_NODES = 6250
        N_EDGES = 200000
        IN_CH = 256
        ADAPTER = 64
        EDGE_DIM = 32
        key = jax.random.key(seed)
        ks = jax.random.split(key, 12)
        s = lambda k, shape: jax.random.normal(k, shape, dtype=jnp.float32) * 0.05
        x = jax.random.normal(ks[0], (N_NODES, IN_CH), dtype=jnp.float32)
        edge_index = jax.random.randint(ks[1], (2, N_EDGES), 0, N_NODES, dtype=jnp.int64)
        edge_attr = jax.random.normal(ks[2], (N_EDGES, EDGE_DIM), dtype=jnp.float32)
        return {'x': x, 'edge_index': edge_index, 'edge_attr': edge_attr, 'W_down': s(ks[3], (ADAPTER, IN_CH)), 'b_down': jnp.zeros((ADAPTER,), jnp.float32), 'W_time': s(ks[4], (ADAPTER, EDGE_DIM)), 'b_time': jnp.zeros((ADAPTER,), jnp.float32), 'W_fusion': s(ks[5], (ADAPTER, 2 * ADAPTER)), 'b_fusion': jnp.zeros((ADAPTER,), jnp.float32), 'W_up': s(ks[6], (IN_CH, ADAPTER)), 'b_up': jnp.zeros((IN_CH,), jnp.float32)}
    _L0_gnn_all = _L0_gnn_setup()
    _L0_gnn_in = {k: v for k, v in _L0_gnn_all.items() if k in ('W_down', 'b_down', 'W_time', 'b_time', 'W_fusion', 'b_fusion', 'W_up', 'b_up')}
    del _L0_gnn_all

    def _L0_ffn_setup():
        import jax, jax.numpy as jnp
        import numpy as np
        E, D, H, TOP_K = (6, 256, 256, 2)
        ROUTER_H = D // 2
        key = jax.random.key(seed)
        ks = jax.random.split(key, 12)
        s = 1.0 / np.sqrt(D)
        sh = 1.0 / np.sqrt(H)
        sr = 1.0 / np.sqrt(ROUTER_H)
        return {'features': jax.random.normal(ks[0], (8, 512, D), dtype=jnp.float32), 'router_w1': jax.random.uniform(ks[1], (D, ROUTER_H), jnp.float32, -s, s), 'router_b1': jnp.zeros((ROUTER_H,), jnp.float32), 'router_w2': jax.random.uniform(ks[2], (ROUTER_H, E), jnp.float32, -sr, sr), 'router_b2': jnp.zeros((E,), jnp.float32), 'expert_w1': jax.random.uniform(ks[3], (E, D, H), jnp.float32, -s, s), 'expert_b1': jnp.zeros((E, H), jnp.float32), 'expert_w2': jax.random.uniform(ks[4], (E, H, H), jnp.float32, -sh, sh), 'expert_b2': jnp.zeros((E, H), jnp.float32), 'expert_w3': jax.random.uniform(ks[5], (E, H, D), jnp.float32, -sh, sh), 'expert_b3': jnp.zeros((E, D), jnp.float32)}
    _L0_ffn_all = _L0_ffn_setup()
    _L0_ffn_in = {k: v for k, v in _L0_ffn_all.items() if k in ('router_w1', 'router_b1', 'router_w2', 'router_b2', 'expert_w1', 'expert_b1', 'expert_w2', 'expert_b2', 'expert_w3', 'expert_b3')}
    del _L0_ffn_all

    def _L1_gnn_setup():
        import jax, jax.numpy as jnp
        import numpy as np
        N_NODES = 6250
        D = 256
        L = 2
        N_EDGES = 100000
        NEG_SLOPE = 0.2

        def _gat_conv(h, W_l, al, ar, b, src, dst, n):
            hp = h @ W_l
            el = hp @ al
            er = hp @ ar
            e = jax.nn.leaky_relu(el[src] + er[dst], NEG_SLOPE)
            emax = jax.ops.segment_max(e, dst, num_segments=n)
            ex = jnp.exp(e - emax[dst])
            denom = jax.ops.segment_sum(ex, dst, num_segments=n)
            alpha = ex / denom[dst]
            out = jax.ops.segment_sum(hp[src] * alpha[:, None], dst, num_segments=n)
            return out + b
        key = jax.random.key(seed)
        ks = jax.random.split(key, 8)
        x = jax.random.normal(ks[0], (N_NODES, D), dtype=jnp.float32)
        W = jax.random.normal(ks[1], (L, D, D), dtype=jnp.float32) * (1.0 / np.sqrt(D))
        attn_l = jax.random.normal(ks[2], (L, D), dtype=jnp.float32) * (1.0 / np.sqrt(D))
        attn_r = jax.random.normal(ks[3], (L, D), dtype=jnp.float32) * (1.0 / np.sqrt(D))
        bias = jnp.zeros((L, D), dtype=jnp.float32)
        src = jax.random.randint(ks[4], (N_EDGES,), 0, N_NODES, dtype=jnp.int32)
        dst = jax.random.randint(ks[5], (N_EDGES,), 0, N_NODES, dtype=jnp.int32)
        return {'x': x, 'W': W, 'attn_l': attn_l, 'attn_r': attn_r, 'bias': bias, 'src': src, 'dst': dst}
    _L1_gnn_all = _L1_gnn_setup()
    _L1_gnn_in = {k: v for k, v in _L1_gnn_all.items() if k in ('W', 'attn_l', 'attn_r', 'bias')}
    del _L1_gnn_all

    def _L1_ffn_setup():
        import jax, jax.numpy as jnp
        import numpy as np
        B, N, D = (16, 512, 256)
        NUM_EXPERTS, TOP_K, HEADS = (4, 2, 4)
        N_EDGES = 131072
        LN_EPS = 1e-05

        def _layernorm(x, g, b):
            mu = x.mean(-1, keepdims=True)
            var = ((x - mu) ** 2).mean(-1, keepdims=True)
            return (x - mu) * jax.lax.rsqrt(var + LN_EPS) * g + b

        def _forward(x, edge_index, W_gat, att_src, att_dst, b_gat, ln_gamma, ln_beta, W1, b1, W2, b2):
            Bc, Nc, Dc = x.shape
            M = Bc * Nc
            x_flat = x.reshape(M, Dc)
            h = (x_flat @ W_gat).reshape(M, HEADS, NUM_EXPERTS)
            loops = jnp.arange(M, dtype=edge_index.dtype)
            src = jnp.concatenate([edge_index[0], loops])
            dst = jnp.concatenate([edge_index[1], loops])
            a_src = (h * att_src).sum(-1)
            a_dst = (h * att_dst).sum(-1)
            e = jax.nn.leaky_relu(a_src[src] + a_dst[dst], negative_slope=0.2)
            e_max = jax.ops.segment_max(e, dst, num_segments=M)
            ee = jnp.exp(e - e_max[dst])
            denom = jax.ops.segment_sum(ee, dst, num_segments=M)
            alpha = ee / (denom[dst] + 1e-16)
            msg = h[src] * alpha[:, :, None]
            agg = jax.ops.segment_sum(msg, dst, num_segments=M).reshape(M, HEADS * NUM_EXPERTS) + b_gat
            scores = _layernorm(agg, ln_gamma, ln_beta).reshape(M, HEADS, NUM_EXPERTS).mean(1)
            scores = scores.reshape(Bc, Nc, NUM_EXPERTS)
            topk_s, topk_i = jax.lax.top_k(scores, TOP_K)
            w = jax.nn.softmax(topk_s, axis=-1)
            out = jnp.zeros_like(x)
            for ei in range(NUM_EXPERTS):
                g = jnp.where(topk_i == ei, w, 0.0).sum(-1)
                hh = jax.nn.gelu(x @ W1[ei] + b1[ei], approximate=False)
                out = out + g[..., None] * (hh @ W2[ei] + b2[ei])
            return out
        key = jax.random.key(seed)
        ks = jax.random.split(key, 8)
        s = 0.05
        return {'x': jax.random.normal(ks[0], (B, N, D), jnp.float32), 'W_gat': jax.random.normal(ks[1], (D, HEADS * NUM_EXPERTS), jnp.float32) * s, 'att_src': jax.random.normal(ks[2], (HEADS, NUM_EXPERTS), jnp.float32) * s, 'att_dst': jax.random.normal(ks[3], (HEADS, NUM_EXPERTS), jnp.float32) * s, 'b_gat': jnp.zeros((HEADS * NUM_EXPERTS,), jnp.float32), 'ln_gamma': jnp.ones((HEADS * NUM_EXPERTS,), jnp.float32), 'ln_beta': jnp.zeros((HEADS * NUM_EXPERTS,), jnp.float32), 'W1': jax.random.normal(ks[4], (NUM_EXPERTS, D, 2 * D), jnp.float32) * s, 'b1': jnp.zeros((NUM_EXPERTS, 2 * D), jnp.float32), 'W2': jax.random.normal(ks[5], (NUM_EXPERTS, 2 * D, D), jnp.float32) * s, 'b2': jnp.zeros((NUM_EXPERTS, D), jnp.float32), 'edge_index': jax.random.randint(ks[6], (2, N_EDGES), 0, B * N, jnp.int32)}
    _L1_ffn_all = _L1_ffn_setup()
    _L1_ffn_in = {k: v for k, v in _L1_ffn_all.items() if k in ('W_gat', 'att_src', 'att_dst', 'b_gat', 'ln_gamma', 'ln_beta', 'W1', 'b1', 'W2', 'b2', 'edge_index')}
    del _L1_ffn_all
    return {'x': x, 'src': src, 'dst': dst, 'edge_attr_32': edge_attr_32, 'L0_gnn_W_down': _L0_gnn_in['W_down'], 'L0_gnn_b_down': _L0_gnn_in['b_down'], 'L0_gnn_W_time': _L0_gnn_in['W_time'], 'L0_gnn_b_time': _L0_gnn_in['b_time'], 'L0_gnn_W_fusion': _L0_gnn_in['W_fusion'], 'L0_gnn_b_fusion': _L0_gnn_in['b_fusion'], 'L0_gnn_W_up': _L0_gnn_in['W_up'], 'L0_gnn_b_up': _L0_gnn_in['b_up'], 'L0_ffn_router_w1': _L0_ffn_in['router_w1'], 'L0_ffn_router_b1': _L0_ffn_in['router_b1'], 'L0_ffn_router_w2': _L0_ffn_in['router_w2'], 'L0_ffn_router_b2': _L0_ffn_in['router_b2'], 'L0_ffn_expert_w1': _L0_ffn_in['expert_w1'], 'L0_ffn_expert_b1': _L0_ffn_in['expert_b1'], 'L0_ffn_expert_w2': _L0_ffn_in['expert_w2'], 'L0_ffn_expert_b2': _L0_ffn_in['expert_b2'], 'L0_ffn_expert_w3': _L0_ffn_in['expert_w3'], 'L0_ffn_expert_b3': _L0_ffn_in['expert_b3'], 'L1_gnn_W': _L1_gnn_in['W'], 'L1_gnn_attn_l': _L1_gnn_in['attn_l'], 'L1_gnn_attn_r': _L1_gnn_in['attn_r'], 'L1_gnn_bias': _L1_gnn_in['bias'], 'L1_ffn_W_gat': _L1_ffn_in['W_gat'], 'L1_ffn_att_src': _L1_ffn_in['att_src'], 'L1_ffn_att_dst': _L1_ffn_in['att_dst'], 'L1_ffn_b_gat': _L1_ffn_in['b_gat'], 'L1_ffn_ln_gamma': _L1_ffn_in['ln_gamma'], 'L1_ffn_ln_beta': _L1_ffn_in['ln_beta'], 'L1_ffn_W1': _L1_ffn_in['W1'], 'L1_ffn_b1': _L1_ffn_in['b1'], 'L1_ffn_W2': _L1_ffn_in['W2'], 'L1_ffn_b2': _L1_ffn_in['b2'], 'L1_ffn_edge_index': _L1_ffn_in['edge_index']}

def reference(x, src, dst, edge_attr_32, L0_gnn_W_down, L0_gnn_b_down, L0_gnn_W_time, L0_gnn_b_time, L0_gnn_W_fusion, L0_gnn_b_fusion, L0_gnn_W_up, L0_gnn_b_up, L0_ffn_router_w1, L0_ffn_router_b1, L0_ffn_router_w2, L0_ffn_router_b2, L0_ffn_expert_w1, L0_ffn_expert_b1, L0_ffn_expert_w2, L0_ffn_expert_b2, L0_ffn_expert_w3, L0_ffn_expert_b3, L1_gnn_W, L1_gnn_attn_l, L1_gnn_attn_r, L1_gnn_bias, L1_ffn_W_gat, L1_ffn_att_src, L1_ffn_att_dst, L1_ffn_b_gat, L1_ffn_ln_gamma, L1_ffn_ln_beta, L1_ffn_W1, L1_ffn_b1, L1_ffn_W2, L1_ffn_b2, L1_ffn_edge_index):
    import jax
    import jax.numpy as jnp

    def _L0_gnn_ref(x, edge_index, edge_attr, W_down, b_down, W_time, b_time, W_fusion, b_fusion, W_up, b_up):
        import jax, jax.numpy as jnp
        import numpy as np
        N_NODES = 6250
        N_EDGES = 200000
        IN_CH = 256
        ADAPTER = 64
        EDGE_DIM = 32
        n = x.shape[0]
        node_feat = jax.nn.relu(x @ W_down.T + b_down)
        time_feat = jax.nn.relu(edge_attr @ W_time.T + b_time)
        src = edge_index[0]
        sums = jax.ops.segment_sum(time_feat, src, num_segments=n)
        counts = jax.ops.segment_sum(jnp.ones((time_feat.shape[0],), jnp.float32), src, num_segments=n)
        node_time_feat = sums / jnp.maximum(counts, 1.0)[:, None]
        combined = jnp.concatenate([node_feat, node_time_feat], axis=-1)
        fused = jax.nn.relu(combined @ W_fusion.T + b_fusion)
        out = fused @ W_up.T + b_up
        return x + out

    def _L0_ffn_ref(features, router_w1, router_b1, router_w2, router_b2, expert_w1, expert_b1, expert_w2, expert_b2, expert_w3, expert_b3):
        import jax, jax.numpy as jnp
        import numpy as np
        E, D, H, TOP_K = (6, 256, 256, 2)
        ROUTER_H = D // 2
        rh = jax.nn.relu(features @ router_w1 + router_b1)
        expert_logits = jax.nn.softmax(rh @ router_w2 + router_b2, axis=-1)
        top_w, top_i = jax.lax.top_k(expert_logits, TOP_K)
        routing_weights = jax.nn.softmax(top_w, axis=-1)
        h1 = jax.nn.relu(jnp.einsum('bsd,edh->bseh', features, expert_w1) + expert_b1)
        h2 = jax.nn.relu(jnp.einsum('bseh,ehf->bsef', h1, expert_w2) + expert_b2)
        expert_out = jnp.einsum('bsef,efo->bseo', h2, expert_w3) + expert_b3
        sel = jnp.take_along_axis(expert_out, top_i[:, :, :, None], axis=2)
        combined = jnp.sum(sel * routing_weights[..., None], axis=2)
        return combined

    def _L1_gnn_ref(x, W, attn_l, attn_r, bias, src, dst):
        import jax, jax.numpy as jnp
        import numpy as np
        N_NODES = 6250
        D = 256
        L = 2
        N_EDGES = 100000
        NEG_SLOPE = 0.2

        def _gat_conv(h, W_l, al, ar, b, src, dst, n):
            hp = h @ W_l
            el = hp @ al
            er = hp @ ar
            e = jax.nn.leaky_relu(el[src] + er[dst], NEG_SLOPE)
            emax = jax.ops.segment_max(e, dst, num_segments=n)
            ex = jnp.exp(e - emax[dst])
            denom = jax.ops.segment_sum(ex, dst, num_segments=n)
            alpha = ex / denom[dst]
            out = jax.ops.segment_sum(hp[src] * alpha[:, None], dst, num_segments=n)
            return out + b
        n = x.shape[0]
        loops = jnp.arange(n, dtype=src.dtype)
        src_sl = jnp.concatenate([src, loops])
        dst_sl = jnp.concatenate([dst, loops])
        h = x
        n_layers = W.shape[0]
        for i in range(n_layers):
            h = _gat_conv(h, W[i], attn_l[i], attn_r[i], bias[i], src_sl, dst_sl, n)
            if i < n_layers - 1:
                h = jax.nn.relu(h)
        return h

    def _L1_ffn_ref(x, W_gat, att_src, att_dst, b_gat, ln_gamma, ln_beta, W1, b1, W2, b2, edge_index):
        import jax, jax.numpy as jnp
        import numpy as np
        B, N, D = (16, 512, 256)
        NUM_EXPERTS, TOP_K, HEADS = (4, 2, 4)
        N_EDGES = 131072
        LN_EPS = 1e-05

        def _layernorm(x, g, b):
            mu = x.mean(-1, keepdims=True)
            var = ((x - mu) ** 2).mean(-1, keepdims=True)
            return (x - mu) * jax.lax.rsqrt(var + LN_EPS) * g + b

        def _forward(x, edge_index, W_gat, att_src, att_dst, b_gat, ln_gamma, ln_beta, W1, b1, W2, b2):
            Bc, Nc, Dc = x.shape
            M = Bc * Nc
            x_flat = x.reshape(M, Dc)
            h = (x_flat @ W_gat).reshape(M, HEADS, NUM_EXPERTS)
            loops = jnp.arange(M, dtype=edge_index.dtype)
            src = jnp.concatenate([edge_index[0], loops])
            dst = jnp.concatenate([edge_index[1], loops])
            a_src = (h * att_src).sum(-1)
            a_dst = (h * att_dst).sum(-1)
            e = jax.nn.leaky_relu(a_src[src] + a_dst[dst], negative_slope=0.2)
            e_max = jax.ops.segment_max(e, dst, num_segments=M)
            ee = jnp.exp(e - e_max[dst])
            denom = jax.ops.segment_sum(ee, dst, num_segments=M)
            alpha = ee / (denom[dst] + 1e-16)
            msg = h[src] * alpha[:, :, None]
            agg = jax.ops.segment_sum(msg, dst, num_segments=M).reshape(M, HEADS * NUM_EXPERTS) + b_gat
            scores = _layernorm(agg, ln_gamma, ln_beta).reshape(M, HEADS, NUM_EXPERTS).mean(1)
            scores = scores.reshape(Bc, Nc, NUM_EXPERTS)
            topk_s, topk_i = jax.lax.top_k(scores, TOP_K)
            w = jax.nn.softmax(topk_s, axis=-1)
            out = jnp.zeros_like(x)
            for ei in range(NUM_EXPERTS):
                g = jnp.where(topk_i == ei, w, 0.0).sum(-1)
                hh = jax.nn.gelu(x @ W1[ei] + b1[ei], approximate=False)
                out = out + g[..., None] * (hh @ W2[ei] + b2[ei])
            return out
        return _forward(x, edge_index, W_gat, att_src, att_dst, b_gat, ln_gamma, ln_beta, W1, b1, W2, b2)
    edge_index = jnp.stack([src, dst])
    x = x + _L0_gnn_ref(_layernorm(x, axis=-1), edge_index, edge_attr_32, L0_gnn_W_down, L0_gnn_b_down, L0_gnn_W_time, L0_gnn_b_time, L0_gnn_W_fusion, L0_gnn_b_fusion, L0_gnn_W_up, L0_gnn_b_up)
    x = x + _L0_ffn_ref(_layernorm(x, axis=-1)[None], L0_ffn_router_w1, L0_ffn_router_b1, L0_ffn_router_w2, L0_ffn_router_b2, L0_ffn_expert_w1, L0_ffn_expert_b1, L0_ffn_expert_w2, L0_ffn_expert_b2, L0_ffn_expert_w3, L0_ffn_expert_b3)[0]
    x = x + _L1_gnn_ref(_layernorm(x, axis=-1), L1_gnn_W, L1_gnn_attn_l, L1_gnn_attn_r, L1_gnn_bias, src, dst)
    x = x + _L1_ffn_ref(_layernorm(x, axis=-1)[None], L1_ffn_W_gat, L1_ffn_att_src, L1_ffn_att_dst, L1_ffn_b_gat, L1_ffn_ln_gamma, L1_ffn_ln_beta, L1_ffn_W1, L1_ffn_b1, L1_ffn_W2, L1_ffn_b2, L1_ffn_edge_index)[0]
    return x

_drawn_inputs = setup_inputs


def setup_inputs(seed=0):
    import zlib

    import numpy as np

    out = dict(_drawn_inputs(seed))
    spreads = {'L0_gnn_b_down': (0.0, 0.8),
     'L0_gnn_b_time': (0.0, 0.8),
     'L0_gnn_b_fusion': (0.0, 0.301),
     'L0_gnn_b_up': (0.0, 0.1),
     'L0_ffn_router_b1': (0.0, 0.37),
     'L0_ffn_router_b2': (0.0, 0.1),
     'L0_ffn_expert_b1': (0.0, 0.8),
     'L0_ffn_expert_b2': (0.0, 0.462),
     'L0_ffn_expert_b3': (0.0, 0.1),
     'L1_gnn_bias': (0.0, 0.1),
     'L1_ffn_b_gat': (0.0, 0.1),
     'L1_ffn_ln_gamma': (1.0, 0.2),
     'L1_ffn_ln_beta': (0.0, 0.1),
     'L1_ffn_b1': (0.0, 0.268),
     'L1_ffn_b2': (0.0, 0.1)}
    factors = {'edge_attr_32': 8.0,
     'L0_gnn_W_time': 8.0,
     'L1_gnn_attn_r': 7.358,
     'L1_ffn_att_src': 2.727,
     'L1_ffn_att_dst': 5.114}
    for name, (base, spread) in spreads.items():
        noise = np.random.default_rng([zlib.crc32(name.encode()), seed]).standard_normal(out[name].shape)
        drawn = base * np.exp(spread * noise) if base else spread * noise
        out[name] = jnp.asarray(drawn.astype(out[name].dtype))
    for name, factor in factors.items():
        out[name] = (out[name] * factor).astype(out[name].dtype)
    return out
```

```python
from contextlib import ExitStack

import concourse.bass as bass
from concourse import mybir

ALU = mybir.AluOpType
ACT = mybir.ActivationFunctionType
AX = mybir.AxisListType
F32 = mybir.dt.float32
BF16 = mybir.dt.bfloat16
I32 = mybir.dt.int32

P = 128
N = 6250
D = 256
KT = D // P
NB = -(-N // P)
TAIL = N - (NB - 1) * P
CB = 4
NCH = NB // CB
E0 = 106250
EP, ET = 125, 850
E1 = 131072
FP_, FT = 128, 1024
AD = 64
ED = 32
K = 4
GE = K * P
NG0 = (E0 + NB * (GE - 1)) // GE
NG1 = (E1 + NB * (GE - 1)) // GE
RING = 4
SLOPE = 0.2
BIG = 2.0 ** 100
NX0, NX1 = 6, 4
RH = 128
HID = 512
HEADS = 4
EPS = 1e-5
PADROW = NB * P
assert EP * ET == E0 and FP_ * FT == E1 and NG0 % RING == 0 and NG1 % RING == 0


class Chain:

    def __init__(self, eng, sem):
        self.eng, self.sem, self.n = eng, sem, 0

    def __call__(self, ins):
        ins.then_inc(self.sem, 1)
        self.n = self.n + 1
        self.eng.wait_ge(self.sem, self.n)


class Kernel:
    def __init__(self, nc, ins, out):
        self.nc, self.i, self.out = nc, ins, out
        self.uid = 0
        self.indirect = 0

    def scope(self):
        ctx = ExitStack()
        nc = self.nc
        self.uid += 1
        u = self.uid

        def sb(name, shape, dt=F32):
            return ctx.enter_context(nc.sbuf_tensor(f"{name}_{u}", shape, dt))

        def ps(name, shape, dt=F32):
            bank = 512 if dt == F32 else 1024
            size = 1
            for x in shape[1:]:
                size *= x
            banks = -(-size // bank)
            whole = ctx.enter_context(nc.psum_tensor(f"{name}_{u}", [P, banks * bank], dt))
            t = whole[0:shape[0], 0:size]
            if len(shape) > 2:
                names = "abcd"[:len(shape) - 1]
                t = t.rearrange(f"p ({' '.join(names)}) -> p {' '.join(names)}", **dict(zip(names, shape[1:])))
            return t

        used = []

        def sem(name):
            used.append(ctx.enter_context(nc.semaphore(f"{name}_{u}")))
            return used[-1]

        def pool_sems(n):
            self.indirect += n
            return [self.keep.enter_context(nc.semaphore(f"s_indirect{self.indirect - n + j}")) for j in range(n)]

        def clear():
            with nc.Block() as block:
                @block.sync
                def _(sp):
                    for s in used:
                        sp.sem_clear(s)

        ctx.callback(clear)

        sem.pool = pool_sems
        return ctx, sb, ps, sem

    def setup(self, keep):
        self.keep = keep
        nc, i = self.nc, self.i
        ctx, sb, ps, sem = self.scope()

        def kp(name, shape, dt=F32):
            return keep.enter_context(nc.sbuf_tensor(name, shape, dt))

        self.X = kp("X", [P, NB, D])
        self.ident = kp("ident", [P, P])
        self.identb = kp("identb", [P, P], BF16)
        self.iota = kp("iota", [P, P])
        self.iotab = kp("iotab", [P, P], BF16)
        self.ones = kp("ones", [P, P])
        self.epsc = kp("epsc", [P, 1])
        self.rowid = kp("rowid", [P, 1])
        self.held = kp("held", [P, 1])
        self.giota = kp("giota", [1, max(NG0, NG1)])
        self.lo0 = kp("lo0", [P, ET, 1])
        self.mean = kp("mean", [P, NB])
        self.rstd = kp("rstd", [P, NB])
        self.grp = [kp(f"grp{g}", [1, n], I32) for g, n in enumerate((NG0, NG0, NG1))]
        self.pos = [kp(f"pos{g}", [P, n], I32) for g, n in enumerate((ET, ET, FT))]
        self.pay = [None, kp("pay1", [P, ET, 2], I32), kp("pay2", [P, FT, 2], I32)]
        self.attr_sorted = nc.dram_tensor("attr_sorted", (NG0 * GE, ED + 1), F32).ap()
        self.pay_sorted = [None] + [nc.dram_tensor(f"pay_sorted{g}", (n * GE, 2), I32).ap() for g, n in ((1, NG0), (2, NG1))]
        self.tab_gat = nc.dram_tensor("tab_gat", (PADROW + 1, D + 2), F32).ap()
        self.tab_rt = nc.dram_tensor("tab_rt", (PADROW + 1, 24), F32).ap()
        s_x, s_o, s_fill, s_st = sem("s_x"), sem("s_const"), sem("s_fill"), sem("s_zero")
        zattr = sb("zattr", [P, 8 * (ED + 1)])
        zpay = sb("zpay", [P, 16, 2], I32)
        zrow = sb("zrow", [1, D + 2])
        with ctx, nc.Block() as block:
            @block.vector
            def _(dve):
                c = Chain(dve, s_o)
                c(nc.vector.memset(self.X[:, NB - 1, :], 0.0))
                nc.vector.memset(self.ones[:, :], 1.0)
                nc.vector.memset(self.epsc[:, :], EPS)
                z3 = zattr[:, :].rearrange("p (r c) -> p r c", c=ED + 1)
                c(nc.vector.memset(zattr[:, :], 0.0))
                c(nc.vector.memset(z3[:, :, ED:ED + 1], float(P)))
                c(nc.vector.memset(zpay[:, :, 0:1], PADROW))
                c(nc.vector.memset(zpay[:, :, 1:2].bitcast(F32), float(P)))
                nc.vector.memset(zrow[:, :], 0.0).then_inc(s_fill, 1)

            @block.gpsimd
            def _(pool):
                pool.iota(self.iota[:, :], [[1, P]], base=0, channel_multiplier=0,
                          allow_small_or_imprecise_dtypes=True)
                pool.iota(self.iotab[:, :], [[1, P]], base=0, channel_multiplier=0,
                          allow_small_or_imprecise_dtypes=True)
                pool.iota(self.rowid[:, :], [[1, 1]], base=0, channel_multiplier=1,
                          allow_small_or_imprecise_dtypes=True)
                pool.iota(self.giota[:, :], [[1, max(NG0, NG1)]], base=0, channel_multiplier=0,
                          allow_small_or_imprecise_dtypes=True)
                for m in (self.ident, self.identb):
                    pool.memset(m[:, :], 0.0).then_inc(s_st, 1)
                pool.wait_ge(s_st, 2)
                for m in (self.ident, self.identb):
                    pool.affine_select(out=m[:, :], in_=m[:, :], compare_op=ALU.not_equal, fill=1.0, base=0,
                                       pattern=[[-1, P]], channel_multiplier=1)

            @block.sync
            def _(sp):
                xb = i["x"][0:(NB - 1) * P, :].rearrange("(b p) d -> p b d", p=P)
                for q in range(0, NB - 1, 12):
                    sp.dma_start(self.X[:, q:q + 12, :], xb[:, q:q + 12, :]).then_inc(s_x, 16)
                sp.wait_ge(s_o, 1)
                sp.dma_start(self.X[0:TAIL, NB - 1, :], i["x"][(NB - 1) * P:N, :]).then_inc(s_x, 16)
                sp.wait_ge(s_fill, 1)
                n = 5
                for dst, z, w in ((self.attr_sorted, zattr[:, :], 8 * (ED + 1)),
                                  (self.pay_sorted[1], zpay[:, :, :].rearrange("p a b -> p (a b)"), 32),
                                  (self.pay_sorted[2], zpay[:, :, :].rearrange("p a b -> p (a b)"), 32)):
                    rows = dst.shape[0]
                    v = dst.rearrange("(p r) c -> p (r c)", p=P)
                    reps = v.shape[1] // w
                    sp.dma_start(v.rearrange("p (r w) -> p r w", w=w),
                                 z.unsqueeze(1).to_broadcast([P, reps, w])).then_inc(s_x, 16)
                    n += 1
                sp.dma_start(self.tab_gat[PADROW:PADROW + 1, :], zrow[:, :]).then_inc(s_x, 16)
                sp.dma_start(self.tab_rt[PADROW:PADROW + 1, :], zrow[:, 0:24]).then_inc(s_x, 16)
                sp.wait_ge(s_x, 16 * (n + 2))

    def sort(self, which, scatter=None):
        nc, i = self.nc, self.i
        ctx, sb, ps, sem = self.scope()
        with ctx:
            W = FT if 2 in which else ET
            key, oth = sb("key", [P, len(which), W], I32), sb("oth", [P, len(which), W], I32)
            hi, mask = sb("hi", [P, W], BF16), sb("mask", [P, W], BF16)
            rank, posf, zero = sb("rank", [P, W]), sb("posf", [P, W]), sb("zero", [P, W])
            mi = sb("mi", [P, W], I32)
            tot, base = sb("tot", [P, NB]), sb("base", [P, NB])
            ni, nf, endg, z49 = sb("ni", [P, NB], I32), sb("nf", [P, NB]), sb("endg", [P, NB]), sb("z49", [P, NB])
            gi = sb("gi", [1, max(NG0, NG1)])
            cmp_, gsum = sb("cmp", [1, max(NG0, NG1), NB]), sb("gsum", [1, max(NG0, NG1)])
            lows = sb("lows", [P, P])
            pre = ps("pre", [P, 2, NB])
            s_key, s_c, s_tot, s_pre, s_low = sem("s_key"), sem("s_sort"), sem("s_tot"), sem("s_pre"), sem("s_low")
            block = ctx.enter_context(nc.Block())
            if scatter is not None:
                slots = self.scatter_slots(sb, sem, scatter)

                @block.gpsimd
                def _(pool):
                    self.scatter_pool(pool, slots)

            @block.sync
            def _(sp):
                for n, g in enumerate(which):
                    if g < 2:
                        a, b = (i["src"], i["dst"]) if g == 0 else (i["dst"], i["src"])
                        a, b = (v.rearrange("(p t) -> p t", p=EP) for v in (a, b))
                    else:
                        a, b = (i["L1_ffn_edge_index"][r].rearrange("(p t) -> p t", p=FP_) for r in (1, 0))
                    pp, cc = a.shape
                    sp.dma_start(key[0:pp, n, 0:cc], a).then_inc(s_key, 16)
                    sp.dma_start(oth[0:pp, n, 0:cc], b).then_inc(s_key, 16)
                sp.wait_ge(s_key, 32 * len(which))
                if scatter is not None:
                    self.scatter_sync(sp, slots)

            @block.tensor
            def _(pe):
                for n, g in enumerate(which):
                    pp = EP if g < 2 else FP_
                    pe.wait_ge(s_tot, n + 1)
                    nc.tensor.matmul(pre[:, 0, :], lows[0:pp, :], tot[0:pp, :], start=True, stop=True)
                    nc.tensor.matmul(pre[:, 1, :], self.ones[0:pp, :], tot[0:pp, :], start=True, stop=True).then_inc(s_pre, 1)

            @block.vector
            def _(dve):
                v = nc.vector
                c = Chain(dve, s_c)
                c(v.memset(zero[:, :], 0.0))
                c(v.memset(z49[:, :], 0.0))
                c(v.tensor_tensor(lows[:, :], self.iota[:, :], self.rowid[:, 0:1].to_broadcast([P, P]), ALU.is_gt))
                dve.wait_ge(s_key, 32 * len(which))
                for n, g in enumerate(which):
                    pp, cc, ng = (EP, ET, NG0) if g < 2 else (FP_, FT, NG1)
                    kk, hh, mm = key[0:pp, n, 0:cc], hi[0:pp, 0:cc], mask[0:pp, 0:cc]
                    m2, rk, pf, zz = mi[0:pp, 0:cc], rank[0:pp, 0:cc], posf[0:pp, 0:cc], zero[0:pp, 0:cc]
                    c(v.tensor_scalar(m2, kk, 7, None, ALU.logical_shift_right))
                    c(v.tensor_copy(hh, m2))
                    start = c.n
                    with dve.Fori(0, NB) as b:
                        c.n = start + b
                        c(v.tensor_scalar(mm, hh, self.iota[0:pp, bass.ds(b, 1)], None, ALU.is_equal, ALU.add,
                                          accum_out=tot[0:pp, bass.ds(b, 1)]))
                    c.n = start + NB
                    v.tensor_copy(base[0:pp, :], tot[0:pp, :]).then_inc(s_tot, 1)
                    dve.wait_ge(s_pre, n + 1)
                    c(v.tensor_scalar(ni[:, :], pre[:, 1, :], float(GE - 1), None, ALU.add))
                    c(v.tensor_scalar(ni[:, :], ni[:, :], 9, None, ALU.logical_shift_right))
                    c(v.tensor_copy(nf[:, :], ni[:, :]))
                    c(v.tensor_tensor_scan(endg[:, :], nf[:, :], z49[:, :], 0.0, ALU.add, ALU.add))
                    c(v.tensor_tensor(nf[:, :], endg[:, :], nf[:, :], ALU.subtract))
                    c(v.scalar_tensor_tensor(base[:, :], nf[:, :], float(GE), pre[:, 0, :], ALU.mult, ALU.add))
                    c(v.tensor_copy(pf, zz))
                    start = c.n
                    with dve.Fori(0, NB) as b:
                        c.n = start + 4 * b
                        c(v.tensor_scalar(mm, hh, self.iota[0:pp, bass.ds(b, 1)], None, ALU.is_equal))
                        c(v.tensor_tensor_scan(rk, mm, zz, base[0:pp, bass.ds(b, 1)], ALU.add, ALU.add))
                        c(v.scalar_tensor_tensor(rk, hh, self.iota[0:pp, bass.ds(b, 1)], rk, ALU.is_equal, ALU.mult))
                        c(v.tensor_tensor(pf, pf, rk, ALU.add))
                    c.n = start + 4 * NB
                    c(v.tensor_scalar(rk, pf, 0.0, float(ng * GE + 1), ALU.is_equal, ALU.mult))
                    c(v.scalar_tensor_tensor(pf, pf, -1.0, rk, ALU.add, ALU.add))
                    c(v.tensor_copy(self.pos[g][0:pp, :], pf))
                    c(v.tensor_copy(cmp_[:, 0:ng, :], endg[0:1, :].unsqueeze(1).to_broadcast([1, ng, NB])))
                    c(v.tensor_tensor(cmp_[:, 0:ng, :], self.giota[0:1, 0:ng].unsqueeze(2).to_broadcast([1, ng, NB]),
                                      cmp_[:, 0:ng, :], ALU.is_ge))
                    c(v.tensor_reduce(gsum[:, 0:ng], cmp_[:, 0:ng, :], AX.X, ALU.add))
                    c(v.tensor_scalar(self.grp[g][:, :], gsum[:, 0:ng], float(NB - 1), None, ALU.min))
                    c(v.tensor_scalar(m2, kk, P - 1, None, ALU.bitwise_and))
                    if g == 0:
                        c(v.tensor_copy(self.lo0[0:pp, :, 0], m2))
                    else:
                        c(v.tensor_copy(self.pay[g][0:pp, :, 1].bitcast(F32), m2))
                        c(v.tensor_scalar(self.pay[g][0:pp, :, 0], oth[0:pp, n, 0:cc], N - 1, None, ALU.min))

    def scatter_slots(self, sb, sem, g, part=(0, 1)):
        parts, cols, sc = (EP, ET, 5) if g < 2 else (FP_, FT, 8)
        w = ED + 1 if g == 0 else 2
        pairs = cols // (2 * sc)
        return dict(g=g, parts=parts, sc=sc, lo=int(pairs * part[0]), hi=int(pairs * part[1]),
                    pos=sb(f"sl_pos{g}", [P, 2, sc], I32), row=sb(f"sl_row{g}", [P, 2, sc, w], F32 if g == 0 else I32),
                    held=sem(f"s_sl_held{g}"), loaded=[sem(f"s_sl_loaded{g}{j}") for j in range(2)],
                    done=sem.pool(2))

    def scatter_sync(self, sp, s):
        g, pp, sc = s["g"], s["parts"], s["sc"]
        n = s["hi"] - s["lo"]
        with sp.Fori(0, n) as i:
            for j in range(2):
                col = (i + s["lo"]) * (2 * sc) + j * sc
                sp.wait_ge(s["done"][j], i * (16 * sc))
                sp.dma_start(s["pos"][0:pp, j, :], self.pos[g][0:pp, bass.ds(col, sc)]).then_inc(s["loaded"][j], 16)
                if g == 0:
                    sp.dma_start(s["row"][0:pp, j, :, 0:ED],
                                 self.i["edge_attr_32"].rearrange("(p t) a -> p t a", p=EP)[:, bass.ds(col, sc), :])\
                        .then_inc(s["loaded"][j], 16)
                    sp.dma_start(s["row"][0:pp, j, :, ED:ED + 1], self.lo0[0:pp, bass.ds(col, sc), :],
                                 allow_slow_non_contiguous=True).then_inc(s["loaded"][j], 16)
                else:
                    sp.dma_start(s["row"][0:pp, j, :, :], self.pay[g][0:pp, bass.ds(col, sc), :]).then_inc(s["loaded"][j], 16)

    def hold(self, pool, s_held, n):
        pool.wait_ge(s_held, n)
        self.nc.gpsimd.tensor_tensor(self.held[:, :], self.rowid[:, :], self.rowid[:, :], ALU.add).then_inc(s_held, 1)

    def scatter_pool(self, pool, s):
        g, pp, sc = s["g"], s["parts"], s["sc"]
        out = self.attr_sorted if g == 0 else self.pay_sorted[g]
        loads = 48 if g == 0 else 32
        n = s["hi"] - s["lo"]
        last = pool.to_reg(out.shape[0] - 1)
        with pool.Fori(0, n) as i:
            for j in range(2):
                pool.wait_ge(s["loaded"][j], (i + 1) * loads)
                self.hold(pool, s["held"], 2 * i + j)
                for k in range(sc):
                    pool.indirect_dma_start(
                        out=out, out_offset=bass.IndirectOffsetOnAxis(ap=s["pos"][0:pp, j, k:k + 1], axis=0),
                        in_=s["row"][0:pp, j, k, :], in_offset=None,
                        bounds_check=last, oob_is_err=False).then_inc(s["done"][j], 16)
        for j in range(2):
            pool.wait_ge(s["done"][j], n * 16 * sc)

    def edge_sums(self, acc, scatter=()):
        nc, i = self.nc, self.i
        ctx, sb, ps, sem = self.scope()
        A1 = AD + 1
        with ctx:
            rows = sb("rows", [P, RING, K, ED + 1])
            attr = sb("attr", [P, RING, K * ED])
            attrT = sb("attrT", [P, 2, P])
            tf = sb("tf", [P, 2, K, A1])
            S = sb("S", [P, RING, K, P])
            wt = sb("wt", [P, K * AD])
            bt = sb("bt", [1, K, AD])
            pT, pF, pU = ([ps(f"{x}{n}", [P, 512]) for n in range(2)] for x in ("pT", "pF", "pU"))
            ld = [sem(f"s_ld{j}") for j in range(RING)]
            s_w, s_z, s_at, s_T, s_Tc, s_F, s_tf, s_S, s_U, s_acc = (sem(x) for x in (
                "s_w", "s_z", "s_at", "s_T", "s_Tc", "s_F", "s_tf", "s_S", "s_U", "s_acc"))
            slots = [self.scatter_slots(sb, sem, g, part) for g, part in scatter]
            block = ctx.enter_context(nc.Block())

            rows_v = self.attr_sorted.rearrange("(s p k) c -> p s k c", p=P, k=K)

            @block.sync
            def _(sp):
                for s in slots:
                    self.scatter_sync(sp, s)

            @block.gpsimd
            def _(pool):
                for s in slots:
                    self.scatter_pool(pool, s)

            @block.scalar
            def _(act):
                act.wait_ge(s_z, 3)
                for k in range(K):
                    act.dma_start(wt[k * ED:(k + 1) * ED, k * AD:(k + 1) * AD], i["L0_gnn_W_time"]).then_inc(s_w, 16)
                    act.dma_start(bt[:, k, :], i["L0_gnn_b_time"].rearrange("(a c) -> a c", a=1)).then_inc(s_w, 16)
                def copy_attrT(g, j):
                    act.wait_ge(s_T, g + 1)
                    if g_ge(g, 2):
                        act.wait_ge(s_F, g - 1)
                    nc.scalar.activation(attrT[:, j % 2, :], pT[j % 2][:, 0:P], ACT.Copy).then_inc(s_Tc, 1)

                def group(g, j, turn, more):
                    if more:
                        copy_attrT(g + 1, (j + 1) % RING)
                    act.wait_ge(s_F, g + 1)
                    if g_ge(g, 2):
                        act.wait_ge(s_U, g - 1)
                    nc.scalar.activation(tf[:, j % 2, :, 0:AD],
                                         pF[j % 2][:, 0:K * AD].rearrange("p (k c) -> p k c", k=K), ACT.Relu).then_inc(s_tf, 1)
                    if not isinstance(g, int) or g + RING < NG0:
                        act.wait_ge(s_S, g + 1)
                        load(g + RING, j)

                def load(g, j):
                    act.dma_start(rows[:, j, :, :], rows_v[:, bass.ds(g, 1), :, :].rearrange("p a k c -> p (a k) c"))\
                        .then_inc(ld[j], 16)

                for j in range(RING):
                    load(j, j)
                copy_attrT(0, 0)
                self.ring(act, NG0, group)

            @block.vector
            def _(dve):
                nc.vector.memset(wt[:, :], 0.0).then_inc(s_z, 1)
                nc.vector.memset(tf[:, :, :, AD:A1], 1.0).then_inc(s_z, 1)
                nc.vector.memset(acc[:, :, :], 0.0).then_inc(s_z, 1)
                dve.wait_ge(s_z, 3)

                def add(g, j):
                    blk = dve.value_load(self.grp[0][0:1, bass.ds(g, 1)], min_val=0, max_val=NB - 1)
                    dve.wait_ge(s_U, g + 1)
                    if g_ge(g, 1):
                        dve.wait_ge(s_acc, g)
                    a = acc[:, bass.ds(blk, 1), :].rearrange("p a c -> p (a c)")
                    nc.vector.tensor_tensor(a, a, pU[j % 2][:, 0:A1], ALU.add).then_inc(s_acc, 1)

                def group(g, j, turn, more):
                    dve.wait_ge(ld[j], 16 * (turn + 1))
                    if g_ge(g, RING):
                        dve.wait_ge(s_U, g - (RING - 1))
                    nc.vector.tensor_copy(attr[:, j, :].rearrange("p (k c) -> p k c", k=K),
                                          rows[:, j, :, 0:ED]).then_inc(s_at, 1)
                    for k in range(K):
                        ins = nc.vector.tensor_scalar(S[:, j, k, :], self.iota[:, :], rows[:, j, k, ED:ED + 1],
                                                      None, ALU.is_equal)
                    ins.then_inc(s_S, 1)
                    if g_ge(g, 3):
                        add(g - 3, (j - 3) % RING)

                self.ring(dve, NG0, group)
                add(NG0 - 3, RING - 3)
                add(NG0 - 2, RING - 2)
                add(NG0 - 1, RING - 1)

            @block.tensor
            def _(pe):
                pe.wait_ge(s_w, 32 * K)

                def turned(g, j, turn):
                    pe.wait_ge(s_at, g + 1)
                    if g_ge(g, 2):
                        pe.wait_ge(s_Tc, g - 1)
                    nc.tensor.transpose(pT[j % 2][:, 0:P], attr[:, j, :], self.ident[:, :]).then_inc(s_T, 1)

                def sums(g, j):
                    pe.wait_ge(s_tf, g + 1)
                    pe.wait_ge(s_S, g + 1)
                    if g_ge(g, 2):
                        pe.wait_ge(s_acc, g - 1)
                    for k in range(K):
                        ins = nc.tensor.matmul(pU[j % 2][:, 0:A1], S[:, j, k, :], tf[:, j % 2, k, :],
                                               start=(k == 0), stop=(k == K - 1))
                    ins.then_inc(s_U, 1)

                def group(g, j, turn, more):
                    if more:
                        turned(g + 1, (j + 1) % RING, turn + (j + 1) // RING)
                    pe.wait_ge(s_Tc, g + 1)
                    if g_ge(g, 2):
                        pe.wait_ge(s_tf, g - 1)
                    nc.tensor.matmul(pF[j % 2][:, 0:K * AD], self.ones[0:1, :], bt[:, :, :].rearrange("a k c -> a (k c)"),
                                     start=True, stop=False)
                    nc.tensor.matmul(pF[j % 2][:, 0:K * AD], attrT[:, j % 2, :], wt[:, :],
                                     start=False, stop=True).then_inc(s_F, 1)
                    if g_ge(g, 1):
                        sums(g - 1, (j - 1) % RING)

                turned(0, 0, 0)
                self.ring(pe, NG0, group)
                sums(NG0 - 1, RING - 1)

    def ring(self, eng, n, group):
        turns = n // RING
        for j in range(RING):
            group(j, j, 0, True)
        with eng.Fori(1, turns - 1) as t:
            for j in range(RING):
                group(t * RING + j, j, t, True)
        for j in range(RING):
            g = (turns - 1) * RING + j
            group(g, j, turns - 1, g < n - 1)


def g_ge(g, n):
    return not isinstance(g, int) or g >= n


def pipeline(eng, n, parts):
    least, most = min(a for a, _ in parts), max(a for a, _ in parts)

    def iteration(it, first=None):
        for ahead, part in parts:
            if first is None:
                g = it + ahead
                if 0 <= g < n:
                    part(g, g % RING, g // RING)
            else:
                t, j = first
                slot, carry = (j + ahead) % RING, (j + ahead) // RING
                part(t * RING + (j + ahead), slot, t + carry)

    for it in range(-most, 2 * RING):
        iteration(it)
    with eng.Fori(2, n // RING - 1) as t:
        for j in range(RING):
            iteration(None, (t, j))
    for it in range(n - RING, n - least):
        iteration(it)


def attention(self, gi, H, F, table, acc, m, adst):
    nc = self.nc
    v = nc.vector
    NG = NG0 if gi == 1 else NG1
    R = table.shape[1]
    FH = F // H
    grp = self.grp[gi]
    ctx, sb, ps, sem = self.scope()
    with ctx:
        pay = sb("pay", [P, RING, K, 2], I32)
        G = sb("G", [P, RING, K, R])
        B = sb("B", [P, RING, K, P], BF16)
        Wm = sb("Wm", [P, 2, H, K, P])
        ST = sb("ST", [P, 2, K * P], BF16)
        mt, t1, t2, r1 = (sb(x, [P, 2 * H]) for x in ("mt", "t1", "t2", "r1"))
        tab = sb("tab", [P, 2, 2 * H])
        tabs = sb("tabs", [P, 2, 3, 2 * H], BF16)
        dm, alpha = sb("dm", [P, RING, H]), sb("alpha", [P, RING, H])
        z, zl, d, p = (sb(x, [P, 2, K, H]) for x in ("z", "zl", "d", "p"))
        if H == 1:
            Pm = sb("Pm", [P, 2, K, P])
        else:
            S = sb("S", [P, 2, K, P], BF16)
            pf = sb("pf", [P, K, H, FH])
            pr = sb("pr", [P, K * F])
            pfs = sb("pfs", [P, 2, 3, K, F], BF16)
        nW = 2 if H == 1 else 1
        pW = [[ps(f"pW{a}{h}", [P, 512]) for h in range(H)] for a in range(nW)]
        pT = ps("pT", [P, 512], BF16)
        pL = ps("pL", [P, K, 2 * H])
        pU = [ps(f"pU{a}", [P, 512]) for a in range(2)]
        lp = [sem(f"s_pay{j}") for j in range(RING)]
        lg = sem.pool(RING)
        (s_held, s_B, s_Wm, s_T, s_ST, s_W, s_max, s_A, s_tab, s_alpha, s_L, s_Bc, s_d, s_p, s_S, s_rhs, s_U, s_acc) = (
            sem(x) for x in ("s_held", "s_B", "s_Wm", "s_T", "s_ST", "s_W", "s_max", "s_stepA", "s_tab", "s_alpha", "s_L",
                             "s_stepB", "s_d", "s_p", "s_S", "s_rhs", "s_U", "s_acc"))
        pay_v = self.pay_sorted[gi].rearrange("(s p k) c -> p s k c", p=P, k=K)
        block = ctx.enter_context(nc.Block())

        @block.sync
        def _(sp):
            def load(g, j, turn):
                if g_ge(g, RING):
                    sp.wait_ge(s_U, g - (RING - 1))
                sp.dma_start(pay[:, j, :, :], pay_v[:, bass.ds(g, 1), :, :].rearrange("p a k c -> p (a k) c"))\
                    .then_inc(lp[j], 16)

            pipeline(sp, NG, [(0, load)])

        @block.gpsimd
        def _(pool):
            def gather(g, j, turn):
                pool.wait_ge(lp[j], 16 * (turn + 1))
                if g_ge(g, RING):
                    pool.wait_ge(s_U, g - (RING - 1))
                    pool.wait_ge(lg[j], 16 * K * turn)
                self.hold(pool, s_held, g)
                for k in range(K):
                    pool.indirect_dma_start(out=G[:, j, k, :], out_offset=None, in_=table,
                                            in_offset=bass.IndirectOffsetOnAxis(ap=pay[:, j, k, 0:1], axis=0))\
                        .then_inc(lg[j], 16)

            pipeline(pool, NG, [(0, gather)])

        @block.tensor
        def _(pe):
            def turn_masks(g, j, turn):
                pe.wait_ge(s_B, g + 1)
                if g_ge(g, 1):
                    pe.wait_ge(s_ST, g)
                for k in range(K):
                    ins = nc.tensor.transpose(pT[:, k * P:(k + 1) * P], B[:, j, k, :], self.identb[:, :])
                ins.then_inc(s_T, 1)
                pe.wait_ge(s_Wm, g + 1)
                for h in range(H):
                    if H == 1:
                        if g_ge(g, 2):
                            pe.wait_ge(s_max, g - 1)
                    elif g_ge(g, 1):
                        pe.wait_ge(s_max, (g - 1) * H + h + 1)
                    for k in range(K):
                        ins = nc.tensor.transpose(pW[j % nW][h][:, k * P:(k + 1) * P], Wm[:, j % 2, h, k, :],
                                                  self.ident[:, :])
                    ins.then_inc(s_W, 1)

            def lookup(g, j, turn):
                pe.wait_ge(s_tab, g + 1)
                pe.wait_ge(s_ST, g + 1)
                if g_ge(g, 1):
                    pe.wait_ge(s_d, g)
                for k in range(K):
                    for q in range(3):
                        ins = nc.tensor.matmul(pL[:, k, :], ST[:, j % 2, k * P:(k + 1) * P], tabs[:, j % 2, q, :],
                                               start=(q == 0), stop=(q == 2))
                ins.then_inc(s_L, 1)

            def sums(g, j, turn):
                pe.wait_ge(s_rhs, g + 1)
                if H > 1:
                    pe.wait_ge(s_S, g + 1)
                if g_ge(g, 2):
                    pe.wait_ge(s_acc, g - 1)
                for k in range(K):
                    if H == 1:
                        ins = nc.tensor.matmul(pU[j % 2][:, 0:F], Pm[:, j % 2, k, :], G[:, j, k, 0:F],
                                               start=(k == 0), stop=(k == K - 1))
                    else:
                        for q in range(3):
                            ins = nc.tensor.matmul(pU[j % 2][:, 0:F], S[:, j % 2, k, :], pfs[:, j % 2, q, k, :],
                                                   start=(k == 0 and q == 0), stop=(k == K - 1 and q == 2))
                ins.then_inc(s_U, 1)

            pipeline(pe, NG, [(1, turn_masks), (0, lookup), (-1, sums)])

        @block.scalar
        def _(act):
            a = nc.scalar

            def masks(g, j, turn):
                act.wait_ge(s_B, g + 1)
                act.wait_ge(lg[j], 16 * K * (turn + 1))
                if g_ge(g, 2):
                    act.wait_ge(s_W, (g - 1) * H)
                for h in range(H):
                    for k in range(K):
                        ins = a.activation(Wm[:, j % 2, h, k, :], B[:, j, k, :], ACT.Identity,
                                           bias=G[:, j, k, F + h:F + h + 1])
                ins.then_inc(s_Wm, 1)
                act.wait_ge(s_T, g + 1)
                if g_ge(g, 2):
                    act.wait_ge(s_L, g - 1)
                a.activation(ST[:, j % 2, :], pT[:, :], ACT.Copy, bias=1.0, scale=1.0 / BIG).then_inc(s_ST, 1)

            def weights(g, j, turn):
                act.wait_ge(s_d, g + 1)
                if g_ge(g, 2):
                    act.wait_ge(s_rhs, g - 1)
                a.activation(p[:, j % 2, :, :], d[:, j % 2, :, :], ACT.Exp).then_inc(s_p, 1)
                if H > 1:
                    if g_ge(g, 2):
                        act.wait_ge(s_U, g - 1)
                    a.activation(S[:, j % 2, :, :], B[:, j, :, :], ACT.Copy, bias=1.0, scale=1.0 / BIG).then_inc(s_S, 1)

            def rescale(g, j, turn):
                act.wait_ge(s_tab, g + 1)
                if g_ge(g, RING):
                    act.wait_ge(s_acc, g - (RING - 1))
                a.activation(alpha[:, j, :], dm[:, j, :], ACT.Exp).then_inc(s_alpha, 1)

            pipeline(act, NG, [(-1, weights), (1, masks), (0, rescale)])

        @block.vector
        def _(dve):
            cA, cB = Chain(dve, s_A), Chain(dve, s_Bc)

            def masks(g, j, turn):
                dve.wait_ge(lp[j], 16 * (turn + 1))
                if g_ge(g, RING):
                    dve.wait_ge(s_U, g - (RING - 1))
                for k in range(K):
                    ins = v.tensor_scalar(B[:, j, k, :], self.iotab[:, :], pay[:, j, k, 1:2].bitcast(F32), -BIG,
                                          ALU.not_equal, ALU.mult)
                ins.then_inc(s_B, 1)

            def maxima(g, j, turn):
                blk = dve.value_load(grp[0:1, bass.ds(g, 1)], min_val=0, max_val=NB - 1)
                mb, ab = (x[:, bass.ds(blk, 1), :].rearrange("p a h -> p (a h)") for x in (m, adst))
                s = j % 2
                cA.n = 7 * g
                for h in range(H):
                    dve.wait_ge(s_W, g * H + h + 1)
                    v.tensor_reduce(mt[:, h:h + 1], pW[j % nW][h][:, :], AX.X, ALU.max).then_inc(s_max, 1)
                if g_ge(g, 2):
                    dve.wait_ge(s_L, g - 1)
                dve.wait_ge(s_max, (g + 1) * H)
                c = cA
                c(v.tensor_tensor(t1[:, 0:H], mt[:, 0:H], ab, ALU.add))
                c(v.scalar_tensor_tensor(t2[:, 0:H], t1[:, 0:H], SLOPE, t1[:, 0:H], ALU.mult, ALU.max))
                v.tensor_scalar(tab[:, s, 0:H], ab, 0.0, None, ALU.add)
                c(v.tensor_tensor(tab[:, s, H:2 * H], t2[:, 0:H], mb, ALU.max))
                if g_ge(g, RING):
                    dve.wait_ge(s_alpha, g - (RING - 1))
                v.tensor_tensor(dm[:, j, :], mb, tab[:, s, H:2 * H], ALU.subtract)
                c(v.tensor_copy(tabs[:, s, 0, :], tab[:, s, :]))
                c(v.tensor_tensor(r1[:, :], tab[:, s, :], tabs[:, s, 0, :], ALU.subtract))
                c(v.tensor_copy(tabs[:, s, 1, :], r1[:, :]))
                c(v.tensor_tensor(tabs[:, s, 2, :], r1[:, :], tabs[:, s, 1, :], ALU.subtract))
                v.tensor_scalar(mb, tab[:, s, H:2 * H], 0.0, None, ALU.add).then_inc(s_tab, 1)

            def scores(g, j, turn):
                s = j % 2
                cB.n = (2 if H == 1 else 6) * g
                dve.wait_ge(s_L, g + 1)
                asrc = G[:, j, :, F:F + H]
                if g_ge(g, 2):
                    dve.wait_ge(s_p, g - 1)
                cB(v.tensor_tensor(z[:, s, :, :], asrc, pL[:, :, 0:H], ALU.add))
                cB(v.scalar_tensor_tensor(zl[:, s, :, :], z[:, s, :, :], SLOPE, z[:, s, :, :], ALU.mult, ALU.max))
                v.tensor_tensor(d[:, s, :, :], zl[:, s, :, :], pL[:, :, H:2 * H], ALU.subtract).then_inc(s_d, 1)

            def weigh(g, j, turn):
                s = j % 2
                dve.wait_ge(s_p, g + 1)
                if g_ge(g, 2):
                    dve.wait_ge(s_U, g - 1)
                if H == 1:
                    for k in range(K):
                        ins = v.tensor_scalar(Pm[:, s, k, :], self.iota[:, :], pay[:, j, k, 1:2].bitcast(F32),
                                              p[:, s, k, 0:1], ALU.is_equal, ALU.mult)
                    ins.then_inc(s_rhs, 1)
                else:
                    cB.n = 6 * g + 2
                    c = cB
                    pff = pf[:, :, :, :].rearrange("p k h f -> p (k h f)")
                    q = [pfs[:, s, i, :, :].rearrange("p k f -> p (k f)") for i in range(3)]
                    for k in range(K):
                        ins = v.tensor_tensor(pf[:, k, :, :], G[:, j, k, 0:F].rearrange("p (h f) -> p h f", h=H),
                                              p[:, s, k, :].unsqueeze(2).to_broadcast([P, H, FH]), ALU.mult)
                    c(ins)
                    c(v.tensor_copy(q[0], pff))
                    c(v.tensor_tensor(pr[:, :], pff, q[0], ALU.subtract))
                    c(v.tensor_copy(q[1], pr[:, :]))
                    v.tensor_tensor(q[2], pr[:, :], q[1], ALU.subtract).then_inc(s_rhs, 1)

            def accumulate(g, j, turn):
                blk = dve.value_load(grp[0:1, bass.ds(g, 1)], min_val=0, max_val=NB - 1)
                dve.wait_ge(s_U, g + 1)
                dve.wait_ge(s_alpha, g + 1)
                if g_ge(g, 1):
                    dve.wait_ge(s_acc, g)
                ac = acc[:, bass.ds(blk, 1), :].rearrange("p a f -> p (a f)")
                for h in range(H):
                    ah = ac[:, h * FH:(h + 1) * FH]
                    ins = v.scalar_tensor_tensor(ah, ah, alpha[:, j, h:h + 1], pU[j % 2][:, h * FH:(h + 1) * FH],
                                                 ALU.mult, ALU.add)
                ins.then_inc(s_acc, 1)

            pipeline(dve, NG, [(2, masks), (-1, scores), (0, maxima), (-1, weigh), (-3, accumulate)])


Kernel.attention = attention


def chunks(eng, body):
    for c in range(2):
        body(c, c, CB, 0)
    with eng.Fori(1, NCH // 2) as t:
        for s in range(2):
            body(t * 2 + s, s, CB, t)
    body(NCH, 0, NB % CB, NCH // 2)


def blk(x, b):
    return x[:, bass.ds(b, 1), :].rearrange("p a d -> p (a d)")


def row(v):
    return v.rearrange("(a c) -> a c", a=1)


def load_all(eng, loads, done):
    for dst, src in loads:
        eng.dma_start(dst, src).then_inc(done, 16)
    eng.wait_ge(done, 16 * len(loads))


def ln_stats(self):
    nc = self.nc
    v = nc.vector
    ctx, sb, ps, sem = self.scope()
    with ctx:
        st = sb("st", [P, NB, 6])
        dl, var = sb("dl", [P, NB]), sb("var", [P, NB])
        s_c, s_var, s_std = sem("s_stat"), sem("s_var"), sem("s_std")
        block = ctx.enter_context(nc.Block())

        @block.vector
        def _(dve):
            c = Chain(dve, s_c)
            with dve.Fori(0, NB - 1) as b:
                v.bn_stats(blk(st, b), blk(self.X, b))
            c(v.bn_stats(st[:, NB - 1, :], self.X[:, NB - 1, :]))
            me, mo, qe, qo = (st[:, :, i] for i in (1, 4, 2, 5))
            c(v.tensor_tensor(dl[:, :], me, mo, ALU.add))
            c(v.tensor_scalar(self.mean[:, :], dl[:, :], 0.5, None, ALU.mult))
            c(v.tensor_tensor(dl[:, :], me, mo, ALU.subtract))
            c(v.tensor_tensor(dl[:, :], dl[:, :], dl[:, :], ALU.mult))
            c(v.tensor_tensor(var[:, :], qe, qo, ALU.add))
            c(v.scalar_tensor_tensor(dl[:, :], dl[:, :], D / 4.0, var[:, :], ALU.mult, ALU.add))
            v.tensor_scalar(var[:, :], dl[:, :], 1.0 / D, EPS, ALU.mult, ALU.add).then_inc(s_var, 1)
            dve.wait_ge(s_std, 1)
            v.reciprocal(self.rstd[:, :], dl[:, :])

        @block.scalar
        def _(act):
            act.wait_ge(s_var, 1)
            nc.scalar.activation(dl[:, :], var[:, :], ACT.Sqrt).then_inc(s_std, 1)


def norm_T(self, XT):
    nc = self.nc
    ctx, sb, ps, sem = self.scope()
    with ctx:
        xn = sb("xn", [P, 2, CB, D])
        pX = [ps(f"pX{s}", [P, KT, CB * P]) for s in range(2)]
        s_xn, s_xT, s_XT = sem("s_xn"), sem("s_xT"), sem("s_XT")
        block = ctx.enter_context(nc.Block())

        @block.vector
        def _(dve):
            def chunk(c, s, n, turn=None):
                if g_ge(c, 2):
                    dve.wait_ge(s_xT, c - 1)
                for i in range(n):
                    b = c * CB + i
                    ins = nc.vector.tensor_scalar(xn[:, s, i, :], blk(self.X, b), self.mean[:, bass.ds(b, 1)],
                                                  self.rstd[:, bass.ds(b, 1)], ALU.subtract, ALU.mult)
                ins.then_inc(s_xn, 1)

            chunks(dve, chunk)

        @block.tensor
        def _(pe):
            def chunk(c, s, n, turn=None):
                pe.wait_ge(s_xn, c + 1)
                if g_ge(c, 2):
                    pe.wait_ge(s_XT, c - 1)
                for i in range(n):
                    for k in range(KT):
                        ins = nc.tensor.transpose(pX[s][:, k, i * P:(i + 1) * P], xn[:, s, i, k * P:(k + 1) * P],
                                                  self.ident[:, :])
                ins.then_inc(s_xT, 1)

            chunks(pe, chunk)

        @block.scalar
        def _(act):
            def chunk(c, s, n, turn=None):
                act.wait_ge(s_xT, c + 1)
                for k in range(KT):
                    ins = nc.scalar.activation(XT[:, k, bass.ds(c * (CB * P), n * P)], pX[s][:, k, 0:n * P], ACT.Copy)
                ins.then_inc(s_XT, 1)

            chunks(act, chunk)


def adapter(self, XT, acc0):
    nc, i_ = self.nc, self.i
    v = nc.vector
    ctx, sb, ps, sem = self.scope()
    with ctx:
        wd = sb("wd", [P, KT, AD])
        wf = sb("wf", [2 * AD, AD])
        wu = sb("wu", [AD, D])
        bd, bf, bu = sb("bd", [AD, 1]), sb("bf", [AD, 1]), sb("bu", [P, D])
        rc = sb("rc", [P, NB])
        nt = sb("nt", [P, 2, CB, 2 * AD])
        both = sb("both", [2 * AD, 2, CB * P])
        fu = sb("fu", [AD, 2, CB * P])
        t = sb("t", [P, 2, CB, D])
        pN, pA, pB = ps("pN", [P, CB * P]), ps("pA", [AD, CB * P]), ps("pB", [AD, CB * P])
        pO = [ps(f"pO{s}", [P, CB, D]) for s in range(2)]
        s_w, s_c, s_nt, s_nT, s_nTc, s_nf, s_nfc, s_fu, s_fuc, s_out, s_x = (sem(x) for x in (
            "s_w", "s_rc", "s_nt", "s_nT", "s_nTc", "s_nf", "s_nfc", "s_fu", "s_fuc", "s_out", "s_xsum"))
        s_t = sem("s_t")
        block = ctx.enter_context(nc.Block())

        @block.sync
        def _(sp):
            load_all(sp, [(wd[:, :, :], i_["L0_gnn_W_down"].rearrange("(k p) m -> p k m", p=P)),
                          (wf[:, :], i_["L0_gnn_W_fusion"]),
                          (wu[:, :], i_["L0_gnn_W_up"]),
                          (bd[:, :], i_["L0_gnn_b_down"].rearrange("(p a) -> p a", a=1)),
                          (bf[:, :], i_["L0_gnn_b_fusion"].rearrange("(p a) -> p a", a=1)),
                          (bu[:, :], row(i_["L0_gnn_b_up"]).partition_broadcast(P))], s_w)

        @block.vector
        def _(dve):
            c_ = Chain(dve, s_c)
            c_(v.tensor_scalar(rc[:, :], acc0[:, :, AD], 1.0, None, ALU.max))
            c_(v.reciprocal(rc[:, :], rc[:, :]))
            c_(v.memset(nt[:, :, :, :], 0.0))
            dve.wait_ge(s_w, 96)

            def means(c, s, n, turn=None):
                if g_ge(c, 2):
                    dve.wait_ge(s_nT, c - 1)
                for i in range(n):
                    b = c * CB + i
                    ins = v.tensor_scalar(nt[:, s, i, AD:], acc0[:, bass.ds(b, 1), 0:AD].rearrange("p a d -> p (a d)"),
                                          rc[:, bass.ds(b, 1)], None, ALU.mult)
                ins.then_inc(s_nt, 1)

            def chunk(c, s, n, turn=None):
                means(c, s, n)
                for i in range(n):
                    b = c * CB + i
                    ins = v.tensor_scalar(t[:, s, i, :], blk(self.X, b), self.mean[:, bass.ds(b, 1)],
                                          self.rstd[:, bass.ds(b, 1)], ALU.subtract, ALU.mult)
                ins.then_inc(s_t, 1)
                dve.wait_ge(s_t, c * 3 + 1)
                tt = t[:, s, 0:n, :]
                v.tensor_tensor(tt, tt, bu[:, :].unsqueeze(1).to_broadcast([P, n, D]), ALU.add).then_inc(s_t, 1)
                dve.wait_ge(s_t, c * 3 + 2)
                dve.wait_ge(s_out, c + 1)
                v.tensor_tensor(tt, tt, pO[s][:, 0:n, :], ALU.add).then_inc(s_t, 1)
                dve.wait_ge(s_t, c * 3 + 3)
                xx = self.X[:, bass.ds(c * CB, n), :]
                v.tensor_tensor(xx, xx, tt, ALU.add).then_inc(s_x, 1)

            chunks(dve, chunk)

        @block.tensor
        def _(pe):
            pe.wait_ge(s_w, 96)

            def chunk(c, s, n, turn=None):
                w = n * P
                cols = bass.ds(c * (CB * P), w)
                pe.wait_ge(s_nt, c + 1)
                pe.wait_ge(s_nTc, c)
                for i in range(n):
                    ins = nc.tensor.transpose(pN[:, i * P:(i + 1) * P], nt[:, s, i, :], self.ident[:, :])
                ins.then_inc(s_nT, 1)
                pe.wait_ge(s_nfc, c)
                for k in range(KT):
                    ins = nc.tensor.matmul(pA[:, 0:w], wd[:, k, :], XT[:, k, cols], start=(k == 0), stop=(k == KT - 1))
                ins.then_inc(s_nf, 1)
                pe.wait_ge(s_nTc, c + 1)
                pe.wait_ge(s_nfc, c + 1)
                nc.tensor.matmul(pB[:, 0:w], wf[:, :], both[:, s, 0:w], start=True, stop=True).then_inc(s_fu, 1)
                pe.wait_ge(s_fuc, c + 1)
                if g_ge(c, 2):
                    pe.wait_ge(s_x, c - 1)
                for i in range(n):
                    ins = nc.tensor.matmul(pO[s][:, i, :], fu[:, s, i * P:(i + 1) * P], wu[:, :], start=True, stop=True)
                ins.then_inc(s_out, 1)

            chunks(pe, chunk)

        @block.scalar
        def _(act):
            act.wait_ge(s_w, 96)

            def chunk(c, s, n, turn=None):
                w = n * P
                act.wait_ge(s_nT, c + 1)
                nc.scalar.activation(both[AD:, s, 0:w], pN[AD:, 0:w], ACT.Copy).then_inc(s_nTc, 1)
                act.wait_ge(s_nf, c + 1)
                nc.scalar.activation(both[0:AD, s, 0:w], pA[:, 0:w], ACT.Relu, bias=bd[:, 0:1]).then_inc(s_nfc, 1)
                act.wait_ge(s_fu, c + 1)
                nc.scalar.activation(fu[:, s, 0:w], pB[:, 0:w], ACT.Relu, bias=bf[:, 0:1]).then_inc(s_fuc, 1)

            chunks(act, chunk)


def router0(self, XT, LG):
    nc, i_ = self.nc, self.i
    ctx, sb, ps, sem = self.scope()
    with ctx:
        w1, w2 = sb("w1", [P, KT, RH]), sb("w2", [RH, NX0])
        b1, b2 = sb("b1", [RH, 1]), sb("b2", [P, NX0])
        rh = sb("rh", [RH, 2, CB * P])
        pR, pG = [ps(f"pR{s}", [RH, CB * P]) for s in range(2)], [ps(f"pG{s}", [P, CB, NX0]) for s in range(2)]
        s_w, s_r, s_rc, s_g, s_lg = (sem(x) for x in ("s_w", "s_r", "s_rc", "s_g", "s_lg"))
        block = ctx.enter_context(nc.Block())

        @block.sync
        def _(sp):
            load_all(sp, [(w1[:, :, :], i_["L0_ffn_router_w1"].rearrange("(k p) m -> p k m", p=P)),
                          (w2[:, :], i_["L0_ffn_router_w2"]),
                          (b1[:, :], i_["L0_ffn_router_b1"].rearrange("(p a) -> p a", a=1)),
                          (b2[:, :], row(i_["L0_ffn_router_b2"]).partition_broadcast(P))], s_w)

        @block.tensor
        def _(pe):
            pe.wait_ge(s_w, 64)

            def chunk(c, s, n, turn=None):
                w = n * P
                if g_ge(c, 2):
                    pe.wait_ge(s_rc, c - 1)
                for k in range(KT):
                    ins = nc.tensor.matmul(pR[s][:, 0:w], w1[:, k, :], XT[:, k, bass.ds(c * (CB * P), w)],
                                           start=(k == 0), stop=(k == KT - 1))
                ins.then_inc(s_r, 1)
                pe.wait_ge(s_rc, c + 1)
                if g_ge(c, 2):
                    pe.wait_ge(s_lg, c - 1)
                for i in range(n):
                    ins = nc.tensor.matmul(pG[s][:, i, :], rh[:, s, i * P:(i + 1) * P], w2[:, :], start=True, stop=True)
                ins.then_inc(s_g, 1)

            chunks(pe, chunk)

        @block.scalar
        def _(act):
            act.wait_ge(s_w, 64)

            def chunk(c, s, n, turn=None):
                act.wait_ge(s_r, c + 1)
                if g_ge(c, 2):
                    act.wait_ge(s_g, c - 1)
                nc.scalar.activation(rh[:, s, 0:n * P], pR[s][:, 0:n * P], ACT.Relu, bias=b1[:, 0:1]).then_inc(s_rc, 1)

            chunks(act, chunk)

        @block.vector
        def _(dve):
            dve.wait_ge(s_w, 64)

            def chunk(c, s, n, turn=None):
                dve.wait_ge(s_g, c + 1)
                nc.vector.tensor_tensor(LG[:, bass.ds(c * CB, n), :], pG[s][:, 0:n, :],
                                        b2[:, :].unsqueeze(1).to_broadcast([P, n, NX0]), ALU.add).then_inc(s_lg, 1)

            chunks(dve, chunk)


def gates(self, S, g, E, softmax):
    nc = self.nc
    v = nc.vector
    ctx, sb, ps, sem = self.scope()
    with ctx:
        a, b = sb("a", [P, NB, E]), sb("b", [P, NB, E])
        o = [sb(f"o{q}", [P, NB, E]) for q in range(2)]
        r = sb("r", [P, E])
        m = [sb(f"m{q}", [P, NB]) for q in range(2)]
        k = sb("k", [P, NB])
        s_c, s_e, s_x = sem("s_gates"), sem("s_exp"), sem("s_for_exp")
        block = ctx.enter_context(nc.Block())

        def wide(x):
            return x[:, :].unsqueeze(2).to_broadcast([P, NB, E])

        @block.scalar
        def _(act):
            n = 1
            if softmax:
                act.wait_ge(s_x, 1)
                nc.scalar.activation(S[:, :, :], a[:, :, :], ACT.Exp).then_inc(s_e, 1)
                n = 2
            act.wait_ge(s_x, n)
            nc.scalar.activation(m[1][:, :], m[1][:, :], ACT.Exp).then_inc(s_e, 1)

        @block.vector
        def _(dve):
            c = Chain(dve, s_c)
            n = 1
            c(v.tensor_scalar(r[:, :], self.iota[:, 0:E], -1.0, float(E), ALU.mult, ALU.add))
            if softmax:
                c(v.tensor_reduce(k[:, :], S[:, :, :], AX.X, ALU.max))
                v.tensor_tensor(a[:, :, :], S[:, :, :], wide(k), ALU.subtract).then_inc(s_x, 1)
                dve.wait_ge(s_e, 1)
                c(v.tensor_reduce(k[:, :], S[:, :, :], AX.X, ALU.add))
                c(v.reciprocal(k[:, :], k[:, :]))
                c(v.tensor_tensor(S[:, :, :], S[:, :, :], wide(k), ALU.mult))
                n = 2
            for q in range(2):
                src = S if q == 0 else b
                c(v.tensor_reduce(m[q][:, :], src[:, :, :], AX.X, ALU.max))
                c(v.tensor_tensor(a[:, :, :], src[:, :, :], wide(m[q]), ALU.is_equal))
                c(v.tensor_tensor(a[:, :, :], a[:, :, :], r[:, :].unsqueeze(1).to_broadcast([P, NB, E]), ALU.mult))
                c(v.tensor_reduce(k[:, :], a[:, :, :], AX.X, ALU.max))
                c(v.tensor_tensor(o[q][:, :, :], a[:, :, :], wide(k), ALU.is_equal))
                if q == 0:
                    c(v.scalar_tensor_tensor(b[:, :, :], o[0][:, :, :], -BIG, S[:, :, :], ALU.mult, ALU.add))
            v.tensor_tensor(m[1][:, :], m[1][:, :], m[0][:, :], ALU.subtract).then_inc(s_x, 1)
            dve.wait_ge(s_e, n)
            c(v.tensor_scalar(k[:, :], m[1][:, :], 1.0, None, ALU.add))
            c(v.reciprocal(m[0][:, :], k[:, :]))
            c(v.tensor_tensor(m[1][:, :], m[1][:, :], m[0][:, :], ALU.mult))
            c(v.tensor_tensor(a[:, :, :], o[0][:, :, :], wide(m[0]), ALU.mult))
            c(v.tensor_tensor(b[:, :, :], o[1][:, :, :], wide(m[1]), ALU.mult))
            c(v.tensor_tensor(g[:, :, :], a[:, :, :], b[:, :, :], ALU.add))


def experts(self, XT, g, layers, E, scatter=()):
    nc = self.nc
    v = nc.vector
    hidden, (w_last, b_last) = layers[:-1], layers[-1]
    ctx, sb, ps, sem = self.scope()
    with ctx:
        W, Bc, H, pH = [], [], [], []
        for n, (w, b, f) in enumerate(hidden):
            kt, mt = w.shape[1] // P, w.shape[2] // P
            W.append(sb(f"W{n}", [P, E, kt, mt * P]))
            Bc.append(sb(f"B{n}", [P, E, mt]))
            H.append(sb(f"H{n}", [P, mt, CB * P]))
            pH.append(ps(f"pH{n}", [P, mt, CB * P]))
        kl = w_last.shape[1] // P
        WL, BL = sb("WL", [P, E, kl, D]), sb("BL", [P, E, D])
        t = sb("t", [P, CB, D])
        pO = ps("pO", [P, CB, D])
        s_w, s_wa = sem("s_w"), sem("s_wact")
        s_h, s_hc = [sem(f"s_h{n}") for n in range(len(hidden))], [sem(f"s_hc{n}") for n in range(len(hidden))]
        s_o, s_t, s_y = sem("s_o"), sem("s_t"), sem("s_y")
        slots = [self.scatter_slots(sb, sem, g_, part) for g_, part in scatter]
        loads = []
        for n, (w, b, f) in enumerate(hidden):
            loads += [(W[n][:, e, :, :], w[e].rearrange("(k p) m -> p k m", p=P)) for e in range(E)]
            loads.append((Bc[n][:, :, :], b.rearrange("e (m p) -> p e m", p=P)))
        loads += [(WL[:, e, :, :], w_last[e].rearrange("(k p) m -> p k m", p=P)) for e in range(E)]
        loads.append((BL[:, :, :], b_last.rearrange("e (a d) -> a e d", a=1).partition_broadcast(P).rearrange("q a e d -> q (a e) d")))
        NW = 16 * len(loads)
        block = ctx.enter_context(nc.Block())

        @block.sync
        def _(sp):
            with nc.allow_non_contiguous_dma(reason="biases to the partitions"):
                load_all(sp, loads, s_w)
            for s in slots:
                self.scatter_sync(sp, s)

        @block.gpsimd
        def _(pool):
            for s in slots:
                self.scatter_pool(pool, s)

        def walk(eng, body):
            with eng.Fori(0, NCH) as c:
                for e in range(E):
                    body(c, e, CB)
            for e in range(E):
                body(NCH, e, NB % CB)

        @block.tensor
        def _(pe):
            pe.wait_ge(s_w, NW)

            def layer(n, c, e, nb):
                w = nb * P
                q = c * E + e
                kt, mt = W[n].shape[2], pH[n].shape[1]
                pe.wait_ge(s_hc[n], q)
                if n:
                    pe.wait_ge(s_hc[n - 1], q + 1)
                for m in range(mt):
                    for k in range(kt):
                        rhs = H[n - 1][:, k, 0:w] if n else XT[:, k, bass.ds(c * (CB * P), w)]
                        ins = nc.tensor.matmul(pH[n][:, m, 0:w], W[n][:, e, k, m * P:(m + 1) * P], rhs,
                                               start=(k == 0), stop=(k == kt - 1))
                ins.then_inc(s_h[n], 1)

            def last(c, e, nb):
                q = c * E + e
                pe.wait_ge(s_hc[-1], q + 1)
                pe.wait_ge(s_t, q)
                for i in range(nb):
                    for k in range(kl):
                        ins = nc.tensor.matmul(pO[:, i, :], H[-1][:, k, i * P:(i + 1) * P], WL[:, e, k, :],
                                               start=(k == 0), stop=(k == kl - 1))
                ins.then_inc(s_o, 1)

            def body(c, e, nb, ahead):
                for n in range(1, len(hidden)):
                    layer(n, c, e, nb)
                if ahead is not None:
                    layer(0, *ahead)
                last(c, e, nb)

            layer(0, 0, 0, CB)
            with pe.Fori(0, NCH - 1) as c:
                for e in range(E):
                    body(c, e, CB, (c, e + 1, CB) if e + 1 < E else (c + 1, 0, CB))
            for c, nb in ((NCH - 1, CB), (NCH, NB % CB)):
                for e in range(E):
                    body(c, e, nb, (c, e + 1, nb) if e + 1 < E else (NCH, 0, NB % CB) if c < NCH else None)

        @block.scalar
        def _(act):
            act.wait_ge(s_w, NW)

            def layer(n, c, e, nb):
                q = c * E + e
                act.wait_ge(s_h[n], q + 1)
                act.wait_ge(s_h[n + 1] if n + 1 < len(hidden) else s_o, q)
                for m in range(pH[n].shape[1]):
                    ins = nc.scalar.activation(H[n][:, m, 0:nb * P], pH[n][:, m, 0:nb * P], hidden[n][2],
                                               bias=Bc[n][:, e, m:m + 1])
                ins.then_inc(s_hc[n], 1)

            if len(hidden) == 1:
                walk(act, lambda c, e, nb: layer(0, c, e, nb))
            else:
                walk(act, lambda c, e, nb: [layer(n, c, e, nb) for n in range(len(hidden))])

        @block.vector
        def _(dve):
            dve.wait_ge(s_w, NW)

            def body(c, e, nb):
                q = c * E + e
                dve.wait_ge(s_o, q + 1)
                dve.wait_ge(s_y, q)
                v.tensor_tensor(t[:, 0:nb, :], pO[:, 0:nb, :], BL[:, e, :].unsqueeze(1).to_broadcast([P, nb, D]),
                                ALU.add).then_inc(s_t, 1)
                dve.wait_ge(s_t, q + 1)
                for i in range(nb):
                    b = c * CB + i
                    x = blk(self.X, b)
                    ge = g[:, bass.ds(b, 1), e:e + 1].rearrange("p a e -> p (a e)")
                    ins = v.scalar_tensor_tensor(x, t[:, i, :], ge, x, ALU.mult, ALU.add)
                ins.then_inc(s_y, 1)

            walk(dve, body)


def gat_tables(self, layer, acc, m, adst):
    nc, i_ = self.nc, self.i
    v = nc.vector
    ctx, sb, ps, sem = self.scope()
    with ctx:
        w = sb("w", [P, KT, D])
        al, ar, bb = sb("al", [P, D]), sb("ar", [P, D]), sb("bb", [P, D])
        rd = sb("rd", [P, NB])
        h = sb("h", [P, 2, CB, D])
        hT = sb("hT", [P, 2, KT, CB * P])
        rows = sb("rows", [P, 2, CB, D + 2])
        el, er, junk, ts, tl = sb("el", [P, 2, CB]), sb("er", [P, 2, CB]), sb("junk", [P, D]), sb("ts", [P, CB]), sb("tl", [P, CB])
        pX = ps("pX", [P, KT, CB * P])
        pO = [ps(f"pO{s}", [P, CB, D]) for s in range(2)]
        s_w, s_c, s_h, s_hr, s_hT, s_hTc, s_o, s_rows, s_ts, s_done, s_st, s_rd = (sem(x) for x in (
            "s_w", "s_c", "s_h", "s_hr", "s_hT", "s_hTc", "s_o", "s_rows", "s_ts", "s_done", "s_stored", "s_rd"))
        sts = [sem(f"s_stored{s}") for s in range(2)]
        block = ctx.enter_context(nc.Block())
        bl = i_["L1_gnn_bias"]

        @block.sync
        def _(sp):
            load_all(sp, [(w[:, :, :], i_["L1_gnn_W"][layer].rearrange("(k p) m -> p k m", p=P)),
                          (al[:, :], i_["L1_gnn_attn_l"][layer:layer + 1, :].partition_broadcast(P)),
                          (ar[:, :], i_["L1_gnn_attn_r"][layer:layer + 1, :].partition_broadcast(P)),
                          (bb[:, :], bl[0:1, :].partition_broadcast(P))], s_w)

            def store(c, s, n, turn=None):
                sp.wait_ge(s_ts, c + 1)
                sp.dma_start(self.tab_gat[bass.ds(c * (CB * P), n * P), :].rearrange("(i p) d -> p i d", p=P),
                             rows[:, s, 0:n, :]).then_inc(sts[s], 16)

            chunks(sp, store)
            sp.wait_ge(sts[0], 16 * (NCH // 2 + 1))
            sp.wait_ge(sts[1], 16 * (NCH // 2))

        @block.vector
        def _(dve):
            dve.wait_ge(s_w, 64)
            c_ = Chain(dve, s_c)
            c_(v.memset(rows[:, :, :, D:D + 1], 1.0))
            if layer:
                c_(v.reciprocal(rd[:, :], acc[:, :, D]))

            def source(c, s, n, turn=None):
                if g_ge(c, 2):
                    dve.wait_ge(s_hT, c - 1)
                for i in range(n):
                    b = c * CB + i
                    if layer:
                        ins = v.scalar_tensor_tensor(h[:, s, i, :], acc[:, bass.ds(b, 1), 0:D].rearrange("p a d -> p (a d)"),
                                                     rd[:, bass.ds(b, 1)], bb[:, :], ALU.mult, ALU.add)
                    else:
                        ins = v.tensor_scalar(h[:, s, i, :], blk(self.X, b), self.mean[:, bass.ds(b, 1)],
                                              self.rstd[:, bass.ds(b, 1)], ALU.subtract, ALU.mult)
                if layer:
                    ins.then_inc(s_hr, 1)
                    dve.wait_ge(s_hr, c + 1)
                    ins = v.tensor_scalar(h[:, s, 0:n, :], h[:, s, 0:n, :], 0.0, None, ALU.max)
                ins.then_inc(s_h, 1)

            def products(c, s, n, turn=None):
                b0 = c * CB
                dve.wait_ge(s_rows, c + 1)
                dve.wait_ge(s_done, c)
                for i in range(n):
                    v.tensor_tensor_reduce(junk[:, :], rows[:, s, i, 0:D], al[:, :], 1.0, 0.0, ALU.mult, ALU.add,
                                           el[:, s, i:i + 1]).then_inc(s_rd, 1)
                    dve.wait_ge(s_rd, c * (2 * CB) + 2 * i + 1)
                    v.tensor_tensor_reduce(junk[:, :], rows[:, s, i, 0:D], ar[:, :], 1.0, 0.0, ALU.mult, ALU.add,
                                           er[:, s, i:i + 1]).then_inc(s_rd, 1)
                    dve.wait_ge(s_rd, c * (2 * CB) + 2 * i + 2)
                v.tensor_tensor(ts[:, 0:n], el[:, s, 0:n], er[:, s, 0:n], ALU.add)
                v.tensor_copy(acc[:, bass.ds(b0, n), :], rows[:, s, 0:n, 0:D + 1])
                v.tensor_scalar(adst[:, bass.ds(b0, n), 0], er[:, s, 0:n], 0.0, None, ALU.add)
                v.tensor_copy(rows[:, s, 0:n, D + 1], el[:, s, 0:n]).then_inc(s_ts, 1)
                dve.wait_ge(s_ts, c + 1)
                v.scalar_tensor_tensor(m[:, bass.ds(b0, n), 0], ts[:, 0:n], SLOPE, ts[:, 0:n], ALU.mult, ALU.max)\
                    .then_inc(s_done, 1)

            source(0, 0, CB)
            with dve.Fori(0, NCH // 2 - 1) as t:
                for s in range(2):
                    source(t * 2 + (s + 1), (s + 1) % 2, CB)
                    products(t * 2 + s, s, CB)
            for c in (NCH - 2, NCH - 1):
                source(c + 1, (c + 1) % 2, CB if c + 1 < NCH else NB % CB)
                products(c, c % 2, CB)
            products(NCH, NCH % 2, NB % CB)

        @block.tensor
        def _(pe):
            pe.wait_ge(s_w, 64)

            def chunk(c, s, n, turn=None):
                pe.wait_ge(s_h, c + 1)
                pe.wait_ge(s_hTc, c)
                for i in range(n):
                    for k in range(KT):
                        ins = nc.tensor.transpose(pX[:, k, i * P:(i + 1) * P], h[:, s, i, k * P:(k + 1) * P],
                                                  self.ident[:, :])
                ins.then_inc(s_hT, 1)
                pe.wait_ge(s_hTc, c + 1)
                if g_ge(c, 2):
                    pe.wait_ge(s_rows, c - 1)
                for i in range(n):
                    for k in range(KT):
                        ins = nc.tensor.matmul(pO[s][:, i, :], hT[:, s, k, i * P:(i + 1) * P], w[:, k, :],
                                               start=(k == 0), stop=(k == KT - 1))
                ins.then_inc(s_o, 1)

            chunks(pe, chunk)

        @block.scalar
        def _(act):
            act.wait_ge(s_w, 64)

            def chunk(c, s, n, turn=None):
                act.wait_ge(s_hT, c + 1)
                for k in range(KT):
                    ins = nc.scalar.activation(hT[:, s, k, 0:n * P], pX[:, k, 0:n * P], ACT.Copy)
                ins.then_inc(s_hTc, 1)
                act.wait_ge(s_o, c + 1)
                if g_ge(c, 2):
                    act.wait_ge(sts[s], 16 * turn)
                    act.wait_ge(s_done, c - 1)
                nc.scalar.activation(rows[:, s, 0:n, 0:D], pO[s][:, 0:n, :], ACT.Copy).then_inc(s_rows, 1)

            chunks(act, chunk)


def finish(self, acc, layer_bias):
    nc = self.nc
    v = nc.vector
    ctx, sb, ps, sem = self.scope()
    with ctx:
        bb, rd = sb("bb", [P, D]), sb("rd", [P, NB])
        s_w, s_t, s_x = sem("s_w"), sem("s_t"), sem("s_x")
        block = ctx.enter_context(nc.Block())

        @block.sync
        def _(sp):
            load_all(sp, [(bb[:, :], layer_bias.partition_broadcast(P))], s_w)

        @block.vector
        def _(dve):
            v.reciprocal(rd[:, :], acc[:, :, D]).then_inc(s_x, 1)
            dve.wait_ge(s_x, 1)
            dve.wait_ge(s_w, 16)

            def block_out(b):
                a = acc[:, bass.ds(b, 1), 0:D].rearrange("p a d -> p (a d)")
                return v.scalar_tensor_tensor(a, a, rd[:, bass.ds(b, 1)], bb[:, :], ALU.mult, ALU.add)

            with dve.Fori(0, NB - 1) as b:
                block_out(b)
            block_out(NB - 1).then_inc(s_t, 1)
            dve.wait_ge(s_t, 1)
            v.tensor_tensor(self.X[:, :, :], self.X[:, :, :], acc[:, :, 0:D], ALU.add)


Kernel.ln_stats = ln_stats
Kernel.norm_T = norm_T
Kernel.adapter = adapter
Kernel.router0 = router0
Kernel.gates = gates
Kernel.experts = experts
Kernel.gat_tables = gat_tables
Kernel.finish = finish


NH = HEADS * NX1
FH1 = NX1 + 1


def router_tables(self, XT, acc, m, adst):
    nc, i_ = self.nc, self.i
    v = nc.vector
    ctx, sb, ps, sem = self.scope()
    with ctx:
        w = sb("w", [P, KT, NH])
        att = [sb(f"att{q}", [P, NH]) for q in range(2)]
        hT = sb("hT", [NH, 2, CB * P])
        H16 = sb("H16", [P, NB, NH])
        rows = sb("rows", [P, NB, HEADS * FH1 + HEADS])
        pr, t = sb("pr", [P, NB, NH]), sb("t", [P, NB, HEADS])
        pH = [ps(f"pH{s}", [NH, CB * P]) for s in range(2)]
        pG = [ps(f"pG{s}", [P, CB, NH]) for s in range(2)]
        s_w, s_h, s_hc, s_g, s_gc, s_c, s_st = (sem(x) for x in ("s_w", "s_h", "s_hc", "s_g", "s_gc", "s_c", "s_stored"))
        s_rows = sem("s_rows")
        block = ctx.enter_context(nc.Block())
        F = HEADS * FH1

        @block.sync
        def _(sp):
            load_all(sp, [(w[:, :, :], i_["L1_ffn_W_gat"].rearrange("(k p) m -> p k m", p=P)),
                          (att[0][:, :], i_["L1_ffn_att_src"].rearrange("(a h) e -> a (h e)", a=1).partition_broadcast(P)),
                          (att[1][:, :], i_["L1_ffn_att_dst"].rearrange("(a h) e -> a (h e)", a=1).partition_broadcast(P))],
                     s_w)
            sp.wait_ge(s_rows, 1)
            sp.dma_start(self.tab_rt[0:PADROW, :].rearrange("(b p) d -> p b d", p=P), rows[:, :, :]).then_inc(s_st, 16)
            sp.wait_ge(s_st, 16)

        @block.tensor
        def _(pe):
            pe.wait_ge(s_w, 48)

            def chunk(c, s, n, turn):
                w_ = n * P
                if g_ge(c, 2):
                    pe.wait_ge(s_hc, c - 1)
                for k in range(KT):
                    ins = nc.tensor.matmul(pH[s][:, 0:w_], w[:, k, :], XT[:, k, bass.ds(c * (CB * P), w_)],
                                           start=(k == 0), stop=(k == KT - 1))
                ins.then_inc(s_h, 1)
                pe.wait_ge(s_hc, c + 1)
                if g_ge(c, 2):
                    pe.wait_ge(s_gc, c - 1)
                for i in range(n):
                    ins = nc.tensor.matmul(pG[s][:, i, :], hT[:, s, i * P:(i + 1) * P], self.ident[0:NH, 0:NH],
                                           start=True, stop=True)
                ins.then_inc(s_g, 1)

            chunks(pe, chunk)

        @block.scalar
        def _(act):
            def chunk(c, s, n, turn):
                act.wait_ge(s_h, c + 1)
                if g_ge(c, 2):
                    act.wait_ge(s_g, c - 1)
                nc.scalar.activation(hT[:, s, 0:n * P], pH[s][:, 0:n * P], ACT.Copy).then_inc(s_hc, 1)

            chunks(act, chunk)

        @block.vector
        def _(dve):
            def chunk(c, s, n, turn):
                dve.wait_ge(s_g, c + 1)
                v.tensor_scalar(H16[:, bass.ds(c * CB, n), :], pG[s][:, 0:n, :], 0.0, None, ALU.add).then_inc(s_gc, 1)

            chunks(dve, chunk)
            c = Chain(dve, s_c)
            dve.wait_ge(s_gc, NCH + 1)
            dve.wait_ge(s_w, 48)
            r4 = rows[:, :, 0:F].rearrange("p b (h f) -> p b h f", h=HEADS)
            for q, out in ((0, rows[:, :, F:F + HEADS]), (1, adst[:, :, :])):
                c(v.tensor_tensor(pr[:, :, :], H16[:, :, :], att[q][:, :].unsqueeze(1).to_broadcast([P, NB, NH]), ALU.mult))
                c(v.tensor_reduce(out, pr[:, :, :].rearrange("p b (h e) -> p b h e", h=HEADS), AX.X, ALU.add))
            c(v.memset(rows[:, :, 0:F], 1.0))
            for h in range(HEADS):
                c(v.tensor_copy(rows[:, :, h * FH1:h * FH1 + NX1], H16[:, :, h * NX1:(h + 1) * NX1]))
            v.tensor_copy(acc[:, :, :], rows[:, :, 0:F]).then_inc(s_rows, 1)
            c(v.tensor_tensor(t[:, :, :], rows[:, :, F:F + HEADS], adst[:, :, :], ALU.add))
            c(v.scalar_tensor_tensor(m[:, :, :], t[:, :, :], SLOPE, t[:, :, :], ALU.mult, ALU.max))


def router_scores(self, acc, S):
    nc, i_ = self.nc, self.i
    v = nc.vector
    ctx, sb, ps, sem = self.scope()
    with ctx:
        bg, ga, be = (sb(x, [P, NH]) for x in ("bg", "ga", "be"))
        A, B = sb("A", [P, NB, NH]), sb("B", [P, NB, NH])
        dn = sb("dn", [P, NB, HEADS])
        mu, var = sb("mu", [P, NB]), sb("var", [P, NB])
        s_w, s_c, s_v, s_s = sem("s_w"), sem("s_c"), sem("s_var"), sem("s_std")
        block = ctx.enter_context(nc.Block())

        @block.sync
        def _(sp):
            load_all(sp, [(t[:, :], row(i_[f"L1_ffn_{n}"]).partition_broadcast(P))
                          for t, n in ((bg, "b_gat"), (ga, "ln_gamma"), (be, "ln_beta"))], s_w)

        @block.scalar
        def _(act):
            act.wait_ge(s_v, 1)
            nc.scalar.activation(mu[:, :], var[:, :], ACT.Sqrt).then_inc(s_s, 1)

        @block.vector
        def _(dve):
            c = Chain(dve, s_c)
            dve.wait_ge(s_w, 48)
            acc4 = acc[:, :, :].rearrange("p b (h f) -> p b h f", h=HEADS)

            def ch(x):
                return x[:, :].unsqueeze(1).to_broadcast([P, NB, NH])

            def per(x):
                return x[:, :].unsqueeze(2).to_broadcast([P, NB, NH])

            c(v.tensor_scalar(dn[:, :, :], acc4[:, :, :, NX1], 1e-16, None, ALU.add))
            c(v.reciprocal(dn[:, :, :], dn[:, :, :]))
            for h in range(HEADS):
                c(v.tensor_tensor(A[:, :, h * NX1:(h + 1) * NX1], acc4[:, :, h, 0:NX1],
                                  dn[:, :, h].unsqueeze(2).to_broadcast([P, NB, NX1]), ALU.mult))
            c(v.tensor_tensor(A[:, :, :], A[:, :, :], ch(bg), ALU.add))
            c(v.tensor_reduce(mu[:, :], A[:, :, :], AX.X, ALU.add))
            c(v.tensor_scalar(mu[:, :], mu[:, :], 1.0 / NH, None, ALU.mult))
            c(v.tensor_tensor(A[:, :, :], A[:, :, :], per(mu), ALU.subtract))
            c(v.tensor_tensor(B[:, :, :], A[:, :, :], A[:, :, :], ALU.mult))
            c(v.tensor_reduce(var[:, :], B[:, :, :], AX.X, ALU.add))
            v.tensor_scalar(var[:, :], var[:, :], 1.0 / NH, EPS, ALU.mult, ALU.add).then_inc(s_v, 1)
            dve.wait_ge(s_s, 1)
            c(v.reciprocal(var[:, :], mu[:, :]))
            c(v.tensor_tensor(A[:, :, :], A[:, :, :], per(var), ALU.mult))
            c(v.tensor_tensor(A[:, :, :], A[:, :, :], ch(ga), ALU.mult))
            c(v.tensor_tensor(A[:, :, :], A[:, :, :], ch(be), ALU.add))
            c(v.tensor_reduce(S[:, :, :], A[:, :, :].rearrange("p b (h e) -> p b e h", h=HEADS), AX.X, ALU.add))
            c(v.tensor_scalar(S[:, :, :], S[:, :, :], 1.0 / HEADS, None, ALU.mult))


def store(self):
    nc = self.nc
    ctx, sb, ps, sem = self.scope()
    with ctx:
        s_out = sem("s_out")
        block = ctx.enter_context(nc.Block())

        @block.sync
        def _(sp):
            ob = self.out[0:(NB - 1) * P, :].rearrange("(b p) d -> p b d", p=P)
            sp.dma_start(ob, self.X[:, 0:NB - 1, :]).then_inc(s_out, 16)
            sp.dma_start(self.out[(NB - 1) * P:N, :], self.X[0:TAIL, NB - 1, :]).then_inc(s_out, 16)
            sp.wait_ge(s_out, 32)


Kernel.router_tables = router_tables
Kernel.router_scores = router_scores
Kernel.store = store


def program(nc, ins, out):
    i = ins
    with ExitStack() as keep:
        k = Kernel(nc, ins, out)
        k.setup(keep)
        k.sort([0])
        k.sort([1, 2], scatter=0)
        k.ln_stats()
        with nc.sbuf_tensor("acc0", [P, NB, AD + 1], F32) as acc0:
            k.edge_sums(acc0, scatter=[(1, (0, 1))])
            with nc.sbuf_tensor("XT0", [P, KT, NB * P], F32) as XT:
                k.norm_T(XT)
                k.adapter(XT, acc0)
        k.ln_stats()
        with nc.sbuf_tensor("XT1", [P, KT, NB * P], F32) as XT, nc.sbuf_tensor("LG0", [P, NB, NX0], F32) as LG, \
                nc.sbuf_tensor("g0", [P, NB, NX0], F32) as g:
            k.norm_T(XT)
            k.router0(XT, LG)
            k.gates(LG, g, NX0, True)
            k.experts(XT, g, [(i["L0_ffn_expert_w1"], i["L0_ffn_expert_b1"], ACT.Relu),
                              (i["L0_ffn_expert_w2"], i["L0_ffn_expert_b2"], ACT.Relu),
                              (i["L0_ffn_expert_w3"], i["L0_ffn_expert_b3"])], NX0, scatter=[(2, (0, 1))])
        k.ln_stats()
        with nc.sbuf_tensor("acc1", [P, NB, D + 1], F32) as acc, nc.sbuf_tensor("m1", [P, NB, 1], F32) as m, \
                nc.sbuf_tensor("adst1", [P, NB, 1], F32) as adst:
            for layer in range(2):
                k.gat_tables(layer, acc, m, adst)
                k.attention(1, 1, D + 1, k.tab_gat, acc, m, adst)
            k.finish(acc, i["L1_gnn_bias"][1:2, :])
        k.ln_stats()
        with nc.sbuf_tensor("XT2", [P, KT, NB * P], F32) as XT, nc.sbuf_tensor("g1", [P, NB, NX1], F32) as g:
            k.norm_T(XT)
            with nc.sbuf_tensor("acc2", [P, NB, HEADS * FH1], F32) as acc, \
                    nc.sbuf_tensor("m2", [P, NB, HEADS], F32) as m, nc.sbuf_tensor("adst2", [P, NB, HEADS], F32) as adst, \
                    nc.sbuf_tensor("S1", [P, NB, NX1], F32) as S:
                k.router_tables(XT, acc, m, adst)
                k.attention(2, HEADS, HEADS * FH1, k.tab_rt, acc, m, adst)
                k.router_scores(acc, S)
                k.gates(S, g, NX1, False)
            k.experts(XT, g, [(i["L1_ffn_W1"], i["L1_ffn_b1"], ACT.Gelu), (i["L1_ffn_W2"], i["L1_ffn_b2"])], NX1)
        k.store()


_TURNED = ("L0_gnn_W_down", "L0_gnn_W_time", "L0_gnn_W_fusion", "L0_gnn_W_up")


def kernel(**inputs):
    import numpy as _np
    import concourse.bacc as _bacc
    from concourse import mybir as _mybir
    from concourse.bass_utils import run_bass_kernel_spmd as _run

    nc = _bacc.Bacc("TRN2", target_bir_lowering=False, num_devices=1)
    arrays, args = {}, {}
    for name in sorted(inputs):
        a = _np.asarray(inputs[name])
        a = _np.ascontiguousarray(a.T if name in _TURNED else a)
        arrays[f"in_{name}_dram"] = a
        args[name] = nc.dram_tensor(f"in_{name}_dram", a.shape, _mybir.dt.from_np(a.dtype), kind="ExternalInput").ap()
    out = nc.dram_tensor("out_dram", (N, D), _mybir.dt.float32, kind="ExternalOutput").ap()
    program(nc, args, out)
    r = _run(nc, [arrays], core_ids=[0])
    return r.results[0]["out_dram"]
```
